# Optimizing a Trainium2 kernel written in Bass

```python
import numpy as np
import jax
import jax.numpy as jnp

def _softmax(x, axis=-1):
    return jax.nn.softmax(x, axis=axis)

def _gelu(x):
    return jax.nn.gelu(x, approximate=True)

def _silu(x):
    return jax.nn.silu(x)

def _sigmoid(x):
    return jax.nn.sigmoid(x)

def _layernorm(x, axis=-1, eps=1e-05):
    m = jnp.mean(x, axis=axis, keepdims=True)
    v = jnp.var(x, axis=axis, keepdims=True)
    return (x - m) / jnp.sqrt(v + eps)

def _scatter_add(tgt, idx, src, axis=0):
    return tgt.at[idx].add(src)

def _segment_sum(src, seg, n):
    return jax.ops.segment_sum(src, seg, n)
kernel_name = 'mk_gnn_preln_d4_gnn_r8_b5bb7b'

def setup_inputs(seed: int=0):
    np.random.seed(seed)
    _w = jnp.asarray

    def _rec_inputs():
        import jax
        import jax.numpy as jnp
        _gk = jax.random.key(seed)
        x = -0.0001006 + 1 * jax.random.normal(jax.random.fold_in(_gk, 1), (12500, 48), jnp.float32)
        src = jax.random.randint(jax.random.fold_in(_gk, 2), (400000,), 0, 12500, jnp.int32)
        dst = jax.random.randint(jax.random.fold_in(_gk, 3), (400000,), 0, 12500, jnp.int32)
        _o = jnp.argsort(dst, stable=True)
        src = src[_o]
        dst = dst[_o]
        edge_attr_40 = jax.random.uniform(jax.random.fold_in(_gk, 13), (400000, 40), jnp.float32, 0.0, 1)
        edge_type_4 = jax.random.randint(jax.random.fold_in(_gk, 15), (400000,), 0, 4, jnp.int32)
        edge_weight = jax.random.uniform(jax.random.fold_in(_gk, 16), (400000,), jnp.float32, 0.0, 6.99999)
        node_type_119 = jax.random.randint(jax.random.fold_in(_gk, 17), (12500,), 0, 119, jnp.int32)
        node_vec = jax.random.uniform(jax.random.fold_in(_gk, 18), (12500,), jnp.float32, 0.0, 1.49999)
        return (x, src, dst, edge_attr_40, edge_type_4, edge_weight, node_type_119, node_vec)
    x, src, dst, edge_attr_40, edge_type_4, edge_weight, node_type_119, node_vec = _rec_inputs()

    def _L0_gnn_setup():
        import jax, jax.numpy as jnp
        import numpy as np
        N_NODES = 12500
        N_EDGES = 200000
        IN_FEAT = 48
        OUT_FEAT = 48
        key = jax.random.key(seed)
        k_h, k_src, k_dst, k_tw, k_tb, k_pw, k_pb = jax.random.split(key, 7)
        lim = 1.0 / np.sqrt(IN_FEAT)
        return {'h': jax.random.normal(k_h, (N_NODES, IN_FEAT), dtype=jnp.float32), 'theta_w': jax.random.uniform(k_tw, (OUT_FEAT, IN_FEAT), jnp.float32, -lim, lim), 'theta_b': jax.random.uniform(k_tb, (OUT_FEAT,), jnp.float32, -lim, lim), 'phi_w': jax.random.uniform(k_pw, (OUT_FEAT, IN_FEAT), jnp.float32, -lim, lim), 'phi_b': jax.random.uniform(k_pb, (OUT_FEAT,), jnp.float32, -lim, lim), 'src': jax.random.randint(k_src, (N_EDGES,), 0, N_NODES, dtype=jnp.int64), 'dst': jax.random.randint(k_dst, (N_EDGES,), 0, N_NODES, dtype=jnp.int64)}
    _L0_gnn_all = _L0_gnn_setup()
    _L0_gnn_in = {k: v for k, v in _L0_gnn_all.items() if k in ('theta_w', 'theta_b', 'phi_w', 'phi_b')}
    del _L0_gnn_all

    def _L1_gnn_setup():
        import jax, jax.numpy as jnp
        import numpy as np
        CUTOFF = 6.0
        LN_EPS = 1e-05
        key = jax.random.key(seed)
        ks = jax.random.split(key, 16)
        N, E, H, R, NEL, G = (6250, 100000, 48, 40, 119, 32)
        inp = {'h': jax.random.normal(ks[0], (N, H), jnp.float32), 'edge_index': jax.random.randint(ks[1], (2, E), 0, N, jnp.int64), 'edge_attr': jax.random.uniform(ks[2], (E, R), jnp.float32), 'distances': jax.random.uniform(ks[3], (E,), jnp.float32) * 7.0, 'atom_z': jax.random.randint(ks[4], (N,), 0, NEL, jnp.int64), 'node_mult': jax.random.uniform(ks[5], (N,), jnp.float32) + 0.5, 'batch': jnp.zeros((N,), jnp.int64), 'W1': jax.random.normal(ks[6], (H, R), jnp.float32) / np.sqrt(R), 'b1': jax.random.normal(ks[7], (H,), jnp.float32) * 0.01, 'W2': jax.random.normal(ks[8], (H, H), jnp.float32) / np.sqrt(H), 'b2': jax.random.normal(ks[9], (H,), jnp.float32) * 0.01, 'emb': jax.random.normal(ks[10], (NEL, G), jnp.float32) * 0.01, 'adaptW': jax.random.normal(ks[11], (G, G), jnp.float32) * 0.01, 'gamma': jnp.ones((H,), jnp.float32), 'beta': jnp.zeros((H,), jnp.float32)}
        return inp
    _L1_gnn_all = _L1_gnn_setup()
    _L1_gnn_in = {k: v for k, v in _L1_gnn_all.items() if k in ('W1', 'b1', 'W2', 'b2', 'emb', 'adaptW', 'gamma', 'beta')}
    del _L1_gnn_all

    def _L2_gnn_setup():
        import jax, jax.numpy as jnp
        import numpy as np
        N_NODES = 12500
        N_EDGES = 200000
        C_IN = 48
        C_OUT = 48
        key = jax.random.key(seed)
        k_x, k_e, k_w = jax.random.split(key, 3)
        x = jax.random.normal(k_x, (N_NODES, C_IN), dtype=jnp.float32)
        edge_index = jax.random.randint(k_e, (2, N_EDGES), 0, N_NODES, dtype=jnp.int64)
        W = jax.random.normal(k_w, (C_IN, C_OUT), dtype=jnp.float32) * (1.0 / np.sqrt(C_IN))
        b = jnp.zeros((C_OUT,), dtype=jnp.float32)
        return {'x': x, 'edge_index': edge_index, 'W': W, 'b': b}
    _L2_gnn_all = _L2_gnn_setup()
    _L2_gnn_in = {k: v for k, v in _L2_gnn_all.items() if k in ('W', 'b')}
    del _L2_gnn_all

    def _L3_gnn_setup():
        import jax, jax.numpy as jnp
        import numpy as np
        N_NODES = 12500
        N_EDGES = 200000
        D_IN = 48
        D_OUT = 48
        N_REL = 4
        key = jax.random.key(seed)
        k1, k2, k3, k4, k5, k6 = jax.random.split(key, 6)
        h = jax.random.normal(k1, (N_NODES, D_IN), dtype=jnp.float32)
        norm_vals = jax.random.uniform(k2, (N_EDGES,), dtype=jnp.float32)
        W = jax.random.normal(k3, (N_REL * D_IN, D_OUT), dtype=jnp.float32) * 0.05
        b = jax.random.normal(k4, (D_OUT,), dtype=jnp.float32) * 0.05
        edge_index = jax.random.randint(k5, (2, N_EDGES), 0, N_NODES, dtype=jnp.int64)
        edge_relation = jax.random.randint(k6, (N_EDGES,), 0, N_REL, dtype=jnp.int32)
        return {'h': h, 'norm_vals': norm_vals, 'W': W, 'b': b, 'edge_index': edge_index, 'edge_relation': edge_relation}
    _L3_gnn_all = _L3_gnn_setup()
    _L3_gnn_in = {k: v for k, v in _L3_gnn_all.items() if k in ('W', 'b')}
    del _L3_gnn_all
    return {'x': x, 'src': src, 'dst': dst, 'edge_attr_40': edge_attr_40, 'edge_type_4': edge_type_4, 'edge_weight': edge_weight, 'node_type_119': node_type_119, 'node_vec': node_vec, 'L0_gnn_theta_w': _L0_gnn_in['theta_w'], 'L0_gnn_theta_b': _L0_gnn_in['theta_b'], 'L0_gnn_phi_w': _L0_gnn_in['phi_w'], 'L0_gnn_phi_b': _L0_gnn_in['phi_b'], 'L1_gnn_W1': _L1_gnn_in['W1'], 'L1_gnn_b1': _L1_gnn_in['b1'], 'L1_gnn_W2': _L1_gnn_in['W2'], 'L1_gnn_b2': _L1_gnn_in['b2'], 'L1_gnn_emb': _L1_gnn_in['emb'], 'L1_gnn_adaptW': _L1_gnn_in['adaptW'], 'L1_gnn_gamma': _L1_gnn_in['gamma'], 'L1_gnn_beta': _L1_gnn_in['beta'], 'L2_gnn_W': _L2_gnn_in['W'], 'L2_gnn_b': _L2_gnn_in['b'], 'L3_gnn_W': _L3_gnn_in['W'], 'L3_gnn_b': _L3_gnn_in['b']}

def reference(x, src, dst, edge_attr_40, edge_type_4, edge_weight, node_type_119, node_vec, L0_gnn_theta_w, L0_gnn_theta_b, L0_gnn_phi_w, L0_gnn_phi_b, L1_gnn_W1, L1_gnn_b1, L1_gnn_W2, L1_gnn_b2, L1_gnn_emb, L1_gnn_adaptW, L1_gnn_gamma, L1_gnn_beta, L2_gnn_W, L2_gnn_b, L3_gnn_W, L3_gnn_b):
    import jax
    import jax.numpy as jnp

    def _L0_gnn_ref(h, theta_w, theta_b, phi_w, phi_b, src, dst):
        import jax, jax.numpy as jnp
        import numpy as np
        N_NODES = 12500
        N_EDGES = 200000
        IN_FEAT = 48
        OUT_FEAT = 48
        phi_all = h @ phi_w.T + phi_b
        diff = h[dst] - h[src]
        e = diff @ theta_w.T + theta_b + phi_all[src]
        out = jax.ops.segment_max(e, dst, num_segments=N_NODES)
        out = jnp.where(jnp.isneginf(out), 0.0, out)
        return out

    def _L1_gnn_ref(h, edge_index, edge_attr, distances, atom_z, node_mult, batch, W1, b1, W2, b2, emb, adaptW, gamma, beta):
        import jax, jax.numpy as jnp
        import numpy as np
        CUTOFF = 6.0
        LN_EPS = 1e-05
        src, dst = (edge_index[0], edge_index[1])
        N = h.shape[0]
        gate = jax.nn.silu(edge_attr @ W1.T + b1) @ W2.T + b2
        ei = emb[atom_z[src]]
        ej = emb[atom_z[dst]]
        adapt_logit = jnp.sum(ei * (ej @ adaptW.T), axis=-1, keepdims=True)
        gate = gate + adapt_logit
        cw = jnp.where(distances < CUTOFF, 0.5 * (jnp.cos(jnp.pi * distances / CUTOFF) + 1.0), 0.0)
        mj = node_mult[dst]
        msg = gate * h[dst] * (cw * mj)[:, None]
        agg = jax.ops.segment_sum(msg, src, num_segments=N)
        tot = jax.ops.segment_sum(mj, src, num_segments=N)
        agg = agg / jnp.clip(tot, 1e-08, None)[:, None]
        x = h + agg
        mu = jnp.mean(x, axis=-1, keepdims=True)
        var = jnp.mean(jnp.square(x - mu), axis=-1, keepdims=True)
        return (x - mu) / jnp.sqrt(var + LN_EPS) * gamma + beta

    def _L2_gnn_ref(x, edge_index, W, b):
        import jax, jax.numpy as jnp
        import numpy as np
        N_NODES = 12500
        N_EDGES = 200000
        C_IN = 48
        C_OUT = 48
        N = x.shape[0]
        loops = jnp.arange(N, dtype=edge_index.dtype)
        src = jnp.concatenate([edge_index[0], loops])
        dst = jnp.concatenate([edge_index[1], loops])
        deg = jax.ops.segment_sum(jnp.ones(src.shape, dtype=x.dtype), dst, num_segments=N)
        dinv = jnp.where(deg > 0, jax.lax.rsqrt(deg), 0.0)
        norm = dinv[src] * dinv[dst]
        h = x @ W
        msg = h[src] * norm[:, None]
        out = jax.ops.segment_sum(msg, dst, num_segments=N)
        return out + b

    def _L3_gnn_ref(h, norm_vals, W, b, edge_index, edge_relation):
        import jax, jax.numpy as jnp
        import numpy as np
        N_NODES = 12500
        N_EDGES = 200000
        D_IN = 48
        D_OUT = 48
        N_REL = 4
        n_nodes = h.shape[0]
        dst = edge_index[0]
        src = edge_index[1]
        hs = h[src]
        outs = []
        for r in range(N_REL):
            w = jnp.where(edge_relation == r, norm_vals, jnp.float32(0.0))
            msg = hs * w[:, None]
            outs.append(jax.ops.segment_sum(msg, dst, num_segments=n_nodes))
        hcat = jnp.concatenate(outs, axis=1)
        return hcat @ W + b
    edge_index = jnp.stack([src, dst])
    batch0 = jnp.zeros((12500,), jnp.int32)
    h = jnp.maximum(_layernorm(x, axis=-1), 0.0)
    x = x + _L0_gnn_ref(h, L0_gnn_theta_w, L0_gnn_theta_b, L0_gnn_phi_w, L0_gnn_phi_b, src, dst)
    h = jnp.maximum(_layernorm(x, axis=-1), 0.0)
    x = x + _L1_gnn_ref(h, edge_index, edge_attr_40, edge_weight, node_type_119, node_vec, batch0, L1_gnn_W1, L1_gnn_b1, L1_gnn_W2, L1_gnn_b2, L1_gnn_emb, L1_gnn_adaptW, L1_gnn_gamma, L1_gnn_beta)
    h = jnp.maximum(_layernorm(x, axis=-1), 0.0)
    x = x + _L2_gnn_ref(h, edge_index, L2_gnn_W, L2_gnn_b)
    h = jnp.maximum(_layernorm(x, axis=-1), 0.0)
    x = x + _L3_gnn_ref(h, edge_weight, L3_gnn_W, L3_gnn_b, edge_index, edge_type_4)
    return x

_drawn_inputs = setup_inputs


def setup_inputs(seed=0):
    import zlib

    import numpy as np

    out = dict(_drawn_inputs(seed))
    spreads = {'L1_gnn_gamma': (1.0, 0.2), 'L1_gnn_beta': (0.0, 0.1), 'L2_gnn_b': (0.0, 0.1)}
    factors = {'edge_attr_40': 8.0,
     'node_vec': 8.0,
     'L1_gnn_b1': 64.0,
     'L1_gnn_b2': 32.825,
     'L1_gnn_emb': 64.0,
     'L1_gnn_adaptW': 64.0,
     'L3_gnn_b': 8.0}
    for name, (base, spread) in spreads.items():
        noise = np.random.default_rng([zlib.crc32(name.encode()), seed]).standard_normal(out[name].shape)
        drawn = base * np.exp(spread * noise) if base else spread * noise
        out[name] = jnp.asarray(drawn.astype(out[name].dtype))
    for name, factor in factors.items():
        out[name] = (out[name] * factor).astype(out[name].dtype)
    return out
```

```python
from contextlib import ExitStack

import concourse.bass as bass
from concourse import mybir

ALU = mybir.AluOpType
ACT = mybir.ActivationFunctionType
F32 = mybir.dt.float32
BF16 = mybir.dt.bfloat16
I32 = mybir.dt.int32
AX = mybir.AxisListType.X

P = 128
H = 48
A = 40
EM = 32
NZ = 119
NR = 4
N = 12500
E = 400000
NB = -(-N // P)
NP = NB * P
LAST = N - (NB - 1) * P
J = E // P
B = 24
NI = J // (2 * B)
TAIL = J - 2 * NI * B
T = 3224
BT = 26
NT = T // (2 * BT)
XR = 3250
ZR = XR // NI
TP = T + 2 * BT
W0 = H + EM
WX = H + 1 + EM
WR = H + 4
FMAX = 3.4028234663852886e38
EPS = 1e-5
PI = 3.141592653589793
JP = J + 2 * B
assert J * P == E and 2 * NI * B + TAIL == J and T >= J + NB and 2 * NT * BT == T
assert ZR * NI == XR and XR >= T and XR * P >= E + NP


class Steps:

    def __init__(self, eng, sem):
        self.eng, self.sem, self.n, self.base = eng, sem, 0, 0

    def __call__(self, ins):
        ins.then_inc(self.sem, 1)
        self.n += 1
        self.eng.wait_ge(self.sem, self.base + self.n)

    def enter(self, i, per_turn):
        self.before, self.per_turn = self.n, per_turn
        self.base, self.n = i * per_turn + self.before, 0

    def leave(self, turns):
        assert self.n == self.per_turn, self.n
        self.base, self.n = 0, self.before + turns * self.per_turn


def bc(ap, dim, n):
    shape = list(ap.shape)
    shape[dim] = n
    return ap.to_broadcast(shape)


def nodes(dram):
    return dram.rearrange("(b p) c -> p b c", p=P)


class Shared:
    pass


def setup(nc, c, sem):
    d, r = c.d, c.r
    s_w, s_res, s_edge, s_edge_free, s_fill, s_iota, s_const, s_v, s_pe = (
        sem(n) for n in ("weight_loaded", "resident_loaded", "edge_loaded", "edge_cleared", "fill", "iota", "const", "setup_dve", "setup_pe"))
    with (
        nc.sbuf_tensor("iota_i", [P, P], I32) as iota_i,
        nc.sbuf_tensor("iota_p", [P, 1], I32) as iota_p,
        nc.sbuf_tensor("len_scratch", [P, J], BF16) as scratch,
        nc.sbuf_tensor("small", [P, 8], F32) as small,
        nc.sbuf_tensor("diag", [P, P], F32) as diag,
        nc.psum_tensor("full_ps", [P, 512], F32) as full_ps,
        nc.Block() as block,
    ):
        @block.sync
        def _(sp):
            sp.dma_start(r.src[:, 0:J], d.src.rearrange("(p j) -> p j", p=P)).then_inc(s_edge, 16)
            sp.dma_start(r.dst[:, 1:], d.dst.rearrange("(p j) -> p j", p=P)).then_inc(s_edge, 16)
            sp.wait_ge(s_edge_free, 1)
            sp.dma_start(r.dst[1:P, 0:1], d.dst.rearrange("(p j) -> p j", p=P)[0:P - 1, J - 1:J]).then_inc(s_edge, 16)
            sp.dma_start(r.w, d.edge_weight.rearrange("(p j) -> p j", p=P)).then_inc(s_w, 16)
            sp.dma_start(r.gidx_i, d.edge_type.rearrange("(p j) -> p j", p=P)).then_inc(s_edge, 16)
            sp.wait_ge(s_const, 4)
            for state in (d.state, d.state2):
                sp.dma_start(state[E:E + P, :], r.ones[:, 0:H]).then_inc(s_w, 16)
            sp.wait_ge(s_w, 48)
            sp.wait_ge(s_edge, 64)

        @block.scalar
        def _(act):
            act.wait_ge(s_fill, 2)
            act.dma_start(r.x[:, 0:NB - 1, :], nodes(d.x[0:(NB - 1) * P, :])).then_inc(s_res, 16)
            act.dma_start(r.x[0:LAST, NB - 1, :], d.x[(NB - 1) * P:N, :]).then_inc(s_res, 16)
            act.dma_start(r.mult[:, 0:NB - 1], d.node_vec[0:(NB - 1) * P].rearrange("(b p) -> p b", p=P)).then_inc(s_res, 16)
            act.dma_start(r.mult[0:LAST, NB - 1:NB], d.node_vec[(NB - 1) * P:N].rearrange("(p o) -> p o", o=1)).then_inc(s_res, 16)
            act.wait_ge(s_res, 64)

        @block.gpsimd
        def _(gp):
            gp.iota(iota_i[:, :], pattern=[[1, P]], base=0, channel_multiplier=0).then_inc(s_iota, 1)
            gp.iota(iota_p[:, :], pattern=[[1, 1]], base=0, channel_multiplier=1).then_inc(s_iota, 1)
            gp.memset(r.ident[:, :], 0.0).then_inc(s_const, 1)
            gp.memset(r.ones[:, :], 1.0).then_inc(s_const, 1)
            gp.wait_ge(s_const, 2)
            gp.affine_select(out=r.ident[:, :], in_=r.ident[:, :], compare_op=ALU.not_equal, fill=1.0, base=0,
                             pattern=[[-1, P]], channel_multiplier=1).then_inc(s_const, 1)
            gp.affine_select(out=r.before[:, :], in_=r.ones[:, :], compare_op=ALU.is_gt, fill=0.0, base=0,
                             pattern=[[1, P]], channel_multiplier=-1).then_inc(s_const, 1)

        @block.vector
        def _(v):
            step = Steps(v, s_v)
            v.memset(r.dst[:, 0:1], -1).then_inc(s_edge_free, 1)
            v.memset(r.x[:, NB - 1, :], 0.0).then_inc(s_fill, 1)
            v.memset(r.mult[:, NB - 1:NB], 0.0).then_inc(s_fill, 1)
            step(v.memset(r.src[:, J:], 0))
            v.wait_ge(s_iota, 2)
            step(v.tensor_copy(r.iota[:, :], iota_i[:, :]))
            step(v.tensor_copy(r.iota16[:, :], iota_i[:, :]))
            step(v.tensor_copy(r.part[:, :], iota_p[:, :]))
            v.wait_ge(s_edge, 64)
            step(v.tensor_tensor(r.same[:, :], r.dst[:, 1:], r.dst[:, 0:J], ALU.is_equal))
            step(v.tensor_copy(small[:, 0:1], r.dst[:, 1:2]))
            step(v.tensor_scalar(scratch[:, :], r.dst[:, 1:], small[:, 0:1], 0.0, ALU.is_equal, ALU.add,
                                 accum_out=small[:, 1:2]))
            step(v.tensor_scalar(small[:, 2:3], small[:, 1:2], float(J), r.same[:, 0:1], ALU.is_equal, ALU.mult))
            step(v.tensor_scalar(small[:, 3:4], r.part[:, :], float(J - 1), small[:, 1:2], ALU.mult, ALU.add))
            step(v.tensor_scalar(small[:, 3:4], small[:, 3:4], -1.0, r.same[:, 0:1], ALU.add, ALU.mult))
            step(v.tensor_scalar(small[:, 4:5], r.same[:, 0:1], -float(E), float(E), ALU.mult, ALU.add))
            step(v.tensor_tensor(small[:, 3:4], small[:, 3:4], r.part[:, :], ALU.add))
            step(v.tensor_copy(r.mend_read[:, :], small[:, 3:4]))
            step(v.tensor_tensor(small[:, 4:5], small[:, 4:5], small[:, 3:4], ALU.add))
            step(v.tensor_copy(r.mend_write[:, :], small[:, 4:5]))
            step(v.tensor_copy(r.first_dst[:, :], r.dst[:, 1:2]))
            step(v.scalar_tensor_tensor(r.gidx, r.dst[:, 1:], float(NR), r.gidx_i, ALU.mult, ALU.add))
            v.wait_ge(s_const, 4)
            step(v.tensor_scalar(diag[:, :], r.ident[:, :], small[:, 2:3], None, ALU.mult))
            v.wait_ge(s_pe, 1)
            step(v.tensor_copy(r.full[:, :], full_ps[0:H, 0:P]))

        @block.tensor
        def _(pe):
            pe.wait_ge(s_v, 18)
            pe.matmul(full_ps[0:H, 0:P], lhsT=r.ones[:, 0:H], rhs=diag[:, :], start=True, stop=True).then_inc(s_pe, 1)


def layernorm_relu(nc, v, step, act_sem, dve_ready, h, x, tmp, stat, relu=True):
    step(v.tensor_reduce(stat[:, 0, :], x, AX, ALU.add))
    step(v.tensor_scalar(stat[:, 0, :], stat[:, 0, :], 1.0 / H, None, ALU.mult))
    step(v.tensor_tensor(h, x, bc(stat[:, 0, :].unsqueeze(2), 2, H), ALU.subtract))
    step(v.tensor_tensor(tmp, h, h, ALU.mult))
    step(v.tensor_reduce(stat[:, 1, :], tmp, AX, ALU.add))
    v.tensor_scalar(stat[:, 1, :], stat[:, 1, :], 1.0 / H, EPS, ALU.mult, ALU.add).then_inc(dve_ready, 1)
    v.wait_ge(*act_sem)
    step(v.reciprocal(stat[:, 3, :], stat[:, 2, :]))
    rstd = bc(stat[:, 3, :].unsqueeze(2), 2, H)
    if relu:
        step(v.scalar_tensor_tensor(h, h, 0.0, rstd, ALU.max, ALU.mult))
    else:
        step(v.tensor_tensor(h, h, rstd, ALU.mult))


def root(nc, act, dve_ready, count, act_sem, stat):
    act.wait_ge(dve_ready, count)
    act.activation(stat[:, 2, :], stat[:, 1, :], ACT.Sqrt).then_inc(act_sem, 1)


class NodeProduct:
    CB = 4
    TURNS = (NB // CB) // 2

    def __init__(self, nc, ctx, sem, name, rhs, width):
        self.rhs, self.width = rhs, width
        self.place = ctx.enter_context(nc.sbuf_tensor(name + "_h", [P, 2, self.CB, H], F32))
        self.hT = ctx.enter_context(nc.sbuf_tensor(name + "_hT", [H, 2, self.CB * P], F32))
        self.tp = [ctx.enter_context(nc.psum_tensor(f"{name}_tp{s}", [H, self.CB * P], F32)) for s in range(2)]
        self.banks = 1 if width <= P else 2
        self.per = self.CB // self.banks
        self.out = [[ctx.enter_context(nc.psum_tensor(f"{name}_o{s}{k}", [P, self.per, 512 // self.per], F32))
                     for k in range(self.banks)] for s in range(2)]
        self.placed, self.turned, self.back, self.made, self.taken, self.pe_go = (
            sem(f"{name}_{n}") for n in ("placed", "turned", "back", "made", "taken", "pe_go"))

    def chunks(self, eng, body):
        with eng.Fori(0, self.TURNS) as i:
            for s in range(2):
                body(i * 2 + s, s, self.CB)
        body(2 * self.TURNS, 0, NB - 2 * self.CB * self.TURNS)

    def on_tensor(self, pe, ident):
        def chunk(g, s, nb):
            pe.wait_ge(self.placed, g + 1)
            pe.wait_ge(self.back, g + 1)
            pe.sem_inc(self.pe_go, 1)
            for b in range(nb):
                last = pe.transpose(self.tp[s][:, b * P:(b + 1) * P], self.place[:, s, b, :], ident[:, :])
            last.then_inc(self.turned, 1)
            pe.wait_ge(self.back, g + 3)
            for b in range(nb):
                k, o = divmod(b, self.per)
                last = pe.matmul(self.out[s][k][:, o, 0:self.width], lhsT=self.hT[:, s, b * P:(b + 1) * P], rhs=self.rhs,
                                 start=True, stop=True)
            last.then_inc(self.made, 1)
        self.chunks(pe, chunk)

    def on_scalar(self, act):
        act.sem_inc(self.back, 2)

        def chunk(g, s, nb):
            act.wait_ge(self.made, g + 1)
            act.wait_ge(self.turned, g + 1)
            act.activation(self.hT[:, s, 0:nb * P], self.tp[s][:, 0:nb * P], ACT.Copy).then_inc(self.back, 1)
        self.chunks(act, chunk)

    def on_vector(self, v, h, take):
        v.sem_inc(self.made, 2)

        def put(g, s, nb):
            v.tensor_scalar(self.place[:, s, 0:nb, :], h[:, bass.ds(g * self.CB, nb), :], 1.0, None, ALU.mult).then_inc(self.placed, 1)

        def get(g, s, nb):
            v.wait_ge(self.made, g + 3)
            rows = [self.out[s][k][:, 0:min(self.per, nb - k * self.per), 0:self.width] for k in range(-(-nb // self.per))]
            take(g, s, nb, rows).then_inc(self.taken, 1)
            v.wait_ge(self.taken, g + 1)
        with v.Fori(0, self.TURNS) as i:
            for s in range(2):
                put(i * 2 + s, s, self.CB)
            for s in range(2):
                get(i * 2 + s, s, self.CB)
        rest = NB - 2 * self.CB * self.TURNS
        put(2 * self.TURNS, 0, rest)
        get(2 * self.TURNS, 0, rest)


def layer0_tables(nc, c, sem):
    d, r = c.d, c.r
    NCH, CB = 7, 14
    CW = CB * P
    with ExitStack() as ctx:
        sb = lambda n, s, t=F32: ctx.enter_context(nc.sbuf_tensor(n, s, t))
        stat = sb("ln_stat", [P, 4, NB])
        wT = sb("w0T", [H, 2 * H])
        phiT = sb("phiT", [H, H])
        bias = sb("bias0", [P, 2, H])
        emb, embT, adT, embs = sb("emb", [NZ, EM]), sb("embT", [EM, NZ]), sb("adaptT", [EM, EM]), sb("embs", [NZ, 2 * EM])
        zrow, zhot = sb("zrow", [NZ, 2, CW], I32), sb("zhot", [NZ, 2, CW])
        rows = sb("rows0", [P, NB, W0])
        zps = [ctx.enter_context(nc.psum_tensor(f"zps{k}", [P, 7, 2 * EM], F32)) for k in range(2)]
        ld, zld, v_s, ready, rt, hs, ps, zh, zm, zt, wr = (
            sem(n) for n in ("l0_weights", "l0_types", "l0_dve", "l0_var", "l0_root", "l0_h", "l0_small_pe", "l0_hot", "l0_hot_mm",
                             "l0_hot_taken", "l0_rows_written"))
        np0 = NodeProduct(nc, ctx, sem, "n0", wT[:, :], 2 * H)
        block = ctx.enter_context(nc.Block())

        @block.sync
        def _(sp):
            sp.dma_start(wT[:, H:], d.theta_w.rearrange("o i -> i o")).then_inc(ld, 16)
            sp.dma_start(phiT[:, :], d.phi_w.rearrange("o i -> i o")).then_inc(ld, 16)
            sp.dma_start(embT[:, :], d.emb.rearrange("z k -> k z")).then_inc(ld, 16)
            sp.dma_start(adT[:, :], d.adaptW.rearrange("o i -> i o")).then_inc(ld, 16)
            sp.dma_start(emb[:, :], d.emb).then_inc(ld, 16)
            sp.dma_start(bias[:, 0, :], bcast_row(d.theta_b)).then_inc(ld, 16)
            sp.dma_start(bias[:, 1, :], bcast_row(d.phi_b)).then_inc(ld, 16)
            for k in range(NCH):
                n = min(CW, N - k * CW)
                if k >= 2:
                    sp.wait_ge(zh, k - 1)
                if n < CW:
                    sp.wait_ge(zt, 1)
                sp.dma_start(zrow[:, k % 2, 0:n], bcast_row(d.node_type[k * CW:k * CW + n], NZ)).then_inc(zld, 16)
                sp.wait_ge(zld, 16 * (k + 1))
            sp.wait_ge(wr, 1)
            sp.dma_start(nodes(d.rows0), rows[:, :, :]).then_inc(ld, 16)
            sp.wait_ge(ld, 16 * 8)

        @block.vector
        def _(v):
            step = Steps(v, v_s)
            layernorm_relu(nc, v, step, (rt, 1), ready, r.a[:, :, :], r.x[:, :, :], rows[:, :, 0:H], stat)
            v.wait_ge(ld, 112)
            step(v.tensor_tensor(wT[:, 0:H], phiT[:, :], wT[:, H:], ALU.subtract))
            step(v.tensor_tensor(bias[:, 0, :], bias[:, 0, :], bias[:, 1, :], ALU.add))
            v.wait_ge(ps, 1)
            step(v.tensor_copy(embs[:, EM:], zps[0][0:NZ, 0, 0:EM]))
            step(v.tensor_copy(embs[:, 0:EM], emb[:, :]))
            v.sem_inc(hs, 1)
            for k in range(NCH):
                if k == NCH - 1:
                    v.memset(zrow[:, k % 2, :], 0).then_inc(zt, 1)
                v.wait_ge(zld, 16 * (k + 1))
                if k >= 2:
                    v.wait_ge(zm, 2 * (k - 1))
                v.tensor_scalar(zhot[:, k % 2, :], zrow[:, k % 2, :], r.part[0:NZ, :], None, ALU.is_equal).then_inc(zh, 1)
                for q in range(2):
                    v.wait_ge(zm, 2 * k + q + 1)
                    b = k * CB + q * 7
                    step(v.tensor_copy(rows[:, b:b + 7, H:], zps[q][:, :, 0:EM]))
                    step(v.tensor_copy(r.e2[:, b:b + 7, :], zps[q][:, :, EM:]))

            def take(g, s, nb, ps_rows):
                v.tensor_scalar(rows[:, bass.ds(g * 4, nb), 0:H], ps_rows[0][:, :, 0:H], 1.0, None, ALU.mult).then_inc(v_s, 1)
                return v.tensor_tensor(r.a[:, bass.ds(g * 4, nb), :], ps_rows[0][:, :, H:], bc(bias[:, 0:1, :], 1, nb), ALU.add)
            np0.on_vector(v, r.a, take)
            v.wait_ge(v_s, step.n + 2 * np0.TURNS + 1)
            v.sem_inc(wr, 1)

        @block.scalar
        def _(act):
            root(nc, act, ready, 1, rt, stat)
            np0.on_scalar(act)

        @block.tensor
        def _(pe):
            pe.wait_ge(ld, 112)
            pe.matmul(zps[0][0:NZ, 0, 0:EM], lhsT=embT[:, :], rhs=adT[:, :], start=True, stop=True).then_inc(ps, 1)
            pe.wait_ge(hs, 1)
            for k in range(NCH):
                pe.wait_ge(zh, k + 1)
                for q in range(2):
                    if k >= 1:
                        pe.wait_ge(v_s, 11 + 4 * (k - 1) + 2 * (q + 1))
                    for b in range(7):
                        o = (q * 7 + b) * P
                        last = pe.matmul(zps[q][:, b, :], lhsT=zhot[:, k % 2, o:o + P], rhs=embs[:, :], start=True, stop=True)
                    last.then_inc(zm, 1)
            np0.on_tensor(pe, r.ident)


def bcast_row(ap, n=P):
    row = ap.rearrange("(o f) -> o f", o=1)
    return row.to_broadcast([n, row.shape[1]])


def gather_reduce(nc, c, sem, name, table, width, state_dram, largest):
    d, r = c.d, c.r
    first = largest
    HB = B // 2
    QB = 4
    TA = NI - NB // 2
    assert TA * 2 * QB >= NB and TA * 2 * QB <= P and NB % 2 == 0
    with ExitStack() as ctx:
        sb = lambda n, s, t=F32: ctx.enter_context(nc.sbuf_tensor(name + n, s, t))
        ring, idx, state, flag = sb("ring", [P, 2, B, width]), sb("idx", [P, 2, B], I32), sb("state", [P, 2, B, H]), sb("flag", [P, 2, B])
        gathered = [sem(f"{name}_gathered{s}") for s in range(2)]
        stored = [sem(f"{name}_state_stored{s}") for s in range(2)]
        kept = [sem(f"{name}_emb_stored{s}") for s in range(2)]
        idx_ready, pool_go, state_ready, emb_ready, dv = (sem(f"{name}_{n}") for n in ("idx_ready", "pool_go", "state_ready", "emb_ready", "dve"))
        if first:
            emb = sb("emb", [P, 2, B, EM])
            hot = sb("hot", [P, 2, HB, P + NB], BF16)
            dsti = sb("dsti", [P, 2, B], I32)
            key, mask, scan = sb("key", [P, J], BF16), sb("mask", [P, J], BF16), sb("scan", [P, J])
            keyi = scan[:, :].bitcast(I32)
            cnt, tot, tiles_i, start, here = sb("cnt", [P, P]), sb("tot", [P, P]), sb("tiles_i", [P, P], I32), sb("start", [P, P]), sb("here", [P, P])
            zero = sb("zero", [P, ZR // 2 * WX])
            zb = sb("zb", [P, P], BF16)
            cnt_ps = ctx.enter_context(nc.psum_tensor(name + "cnt_ps", [P, 512], F32))
            base_ps = ctx.enter_context(nc.psum_tensor(name + "base_ps", [P, 2, 256], F32))
            hot_ready, hot_used, counted, base_made, zeroed, zero_ready, pe_done = (
                sem(f"{name}_{n}") for n in ("hot_ready", "hot_used", "counted", "base_made", "zeroed", "zero_ready", "pe_done"))
        block = ctx.enter_context(nc.Block())

        @block.gpsimd
        def _(gp):
            def gather(s, nb):
                for b in range(nb):
                    gp.indirect_dma_start(ring[:, s, b, :], None, table,
                                          bass.IndirectOffsetOnAxis(ap=idx[:, s, b:b + 1], axis=0)).then_inc(gathered[s], 16)
            with gp.Fori(0, NI) as i:
                for s in range(2):
                    gp.wait_ge(idx_ready, i * 2 + (s + 1))
                    gp.sem_inc(pool_go, 1)
                    gather(s, B)
            gp.wait_ge(idx_ready, 2 * NI + 1)
            gather(0, TAIL)

        @block.sync
        def _(sp):
            state_v = state_dram[0:E, :].rearrange("(p j) c -> p j c", p=P)
            emb_v = d.emb_edge.rearrange("(p j) c -> p j c", p=P) if first else None
            for s in range(2):
                sp.sem_inc(stored[s], 16)
                if first:
                    sp.sem_inc(kept[s], 16)

            def store(g, s, nb):
                if first:
                    sp.wait_ge(emb_ready, g + 1)
                    sp.dma_start(emb_v[:, bass.ds(g * B, nb), :], emb[:, s, 0:nb, :]).then_inc(kept[s], 16)
                sp.wait_ge(state_ready, g + 1)
                sp.dma_start(state_v[:, bass.ds(g * B, nb), :], state[:, s, 0:nb, :]).then_inc(stored[s], 16)
            with sp.Fori(0, NI) as i:
                for s in range(2):
                    store(i * 2 + s, s, B)
            store(2 * NI, 0, TAIL)
            for s in range(2):
                sp.wait_ge(stored[s], 16 * (NI + 2 - s))
                if first:
                    sp.wait_ge(kept[s], 16 * (NI + 2 - s))

        @block.vector
        def _(v):
            step = Steps(v, dv)
            neutral = -FMAX if largest else 0.0
            op0, op1 = (ALU.min, ALU.max) if largest else (ALU.mult, ALU.add)

            def stage(g, s):
                v.tensor_scalar(idx[:, s, :], r.src[:, bass.ds(g * B, B)], 0.0, None, ALU.add).then_inc(idx_ready, 1)

            def reduce(i, s, nb):
                g = i * 2 + s
                if largest:
                    step(v.tensor_scalar(flag[:, s, 0:nb], r.same[:, bass.ds(g * B, nb)], 2.0, -1.0, ALU.mult, ALU.add))
                    step(v.tensor_scalar(flag[:, s, 0:nb], flag[:, s, 0:nb], FMAX, None, ALU.mult))
                else:
                    step(v.tensor_scalar(flag[:, s, 0:nb], r.same[:, bass.ds(g * B, nb)], 1.0, None, ALU.mult))
                v.wait_ge(gathered[s], (i + 1) * (16 * B) if nb == B else NI * 16 * B + 16 * nb)
                v.wait_ge(stored[s], i * 16 + 16)
                for b in range(nb):
                    prev = state[:, s, b - 1, :] if b else state[:, 1 - s, B - 1, :]
                    ins = v.scalar_tensor_tensor(state[:, s, b, :], prev, flag[:, s, b:b + 1], ring[:, s, b, 0:H], op0, op1)
                    step(ins)
                v.sem_inc(state_ready, 1)

            def onehots(i, s, nb, half, n_after):
                g = i * 2 + s
                v.wait_ge(hot_used, i * 4 + (2 * s + half + 1))
                for b in range(half * HB, min(nb, (half + 1) * HB)):
                    v.tensor_scalar(hot[:, half, b - half * HB, 0:P], r.iota16[:, :], dsti[:, 1, b:b + 1], None, ALU.is_equal)
                    v_last = v.tensor_scalar(hot[:, half, b - half * HB, P:], r.iota16[:, 0:NB], dsti[:, 0, b:b + 1], None, ALU.is_equal)
                    yield_last = v_last
                yield_last.then_inc(hot_ready, 1)

            def count(i, s, nb):
                g = i * 2 + s
                for q, (op, val) in enumerate(((ALU.arith_shift_right, 7), (ALU.bitwise_and, P - 1))):
                    step(v.tensor_scalar(dsti[:, q, 0:nb], r.dst[:, bass.ds(g * B + 1, nb)], val, None, op))
                onehots(i, s, nb, 0, None)
                if nb > HB:
                    onehots(i, s, nb, 1, None)

            step(v.memset(state[:, 1, B - 1, :], neutral))
            if first:
                v.memset(zero[:, :], 0.0).then_inc(zero_ready, 1)
            for s in range(2):
                stage(s, s)
            if first:
                v.sem_inc(hot_used, 2)
                step(v.memset(cnt[:, :], 0.0))
                v.memset(zb[:, :], 0.0).then_inc(zero_ready, 1)
                step(v.tensor_scalar(keyi, r.src[:, 0:J], 7, None, ALU.arith_shift_right))
                step(v.tensor_copy(key[:, :], keyi))

            def turn(i, extra):
                for s in range(2):
                    reduce(i, s, B)
                    if first:
                        v.wait_ge(emb_ready, i * 2 + (s + 1))
                    stage((i + 1) * 2 + s, s)
                    if first:
                        count(i, s, B)
                        extra(i, s)

            if not first:
                with v.Fori(0, NI) as i:
                    step.enter(i, 2 * (B + 1))
                    turn(i, None)
                step.leave(NI)
                reduce(NI, 0, TAIL)
            else:
                def count_blocks(i, s):
                    for q in range(QB):
                        b = (i * 2 + s) * QB + q
                        step(v.tensor_scalar(mask[:, :], key[:, :], r.iota[:, bass.ds(b, 1)], 0.0, ALU.is_equal, ALU.add,
                                             accum_out=cnt[:, bass.ds(b, 1)]))

                def rank_block(i, s):
                    b = (i - TA) * 2 + s
                    step(v.tensor_scalar(mask[:, :], key[:, :], r.iota[:, bass.ds(b, 1)], None, ALU.is_equal))
                    step(v.tensor_tensor_scan(scan[:, :], mask[:, :], mask[:, :], here[:, bass.ds(b, 1)], ALU.add, ALU.bypass))
                    step(v.scalar_tensor_tensor(scan[:, :], key[:, :], r.iota[:, bass.ds(b, 1)], scan[:, :], ALU.is_equal, ALU.mult))
                    step(v.tensor_tensor(r.pos, r.pos, scan[:, :], ALU.add))

                with v.Fori(0, TA) as i:
                    step.enter(i, 2 * (B + 4 + QB))
                    turn(i, count_blocks)
                step.leave(TA)
                v.sem_inc(counted, 1)
                v.wait_ge(base_made, 1)
                step(v.tensor_scalar(tot[:, :], base_ps[:, 0, 0:P], float(P - 1), None, ALU.add))
                step(v.tensor_copy(tiles_i[:, :], tot[:, :]))
                step(v.tensor_scalar(tiles_i[:, :], tiles_i[:, :], 7, None, ALU.arith_shift_right))
                step(v.tensor_copy(tot[:, :], tiles_i[:, :]))
                step(v.tensor_scalar(tot[:, :], tot[:, :], 1.0, None, ALU.max))
                step(v.tensor_tensor_scan(start[:, :], tot[:, :], tot[:, :], 0.0, ALU.add, ALU.bypass))
                step(v.tensor_tensor(r.first_tile[:, :], start[:, :], tot[:, :], ALU.subtract))
                step(v.tensor_scalar(start[:, :], r.first_tile[:, :], float(P), -1.0, ALU.mult, ALU.add))
                step(v.tensor_tensor(here[:, :], start[:, :], base_ps[:, 1, 0:P], ALU.add))
                step(v.memset(r.pos, 0.0))
                with v.Fori(TA, NI) as i:
                    step.enter(i - TA, 2 * (B + 4 + 4))
                    turn(i, rank_block)
                step.leave(NI - TA)
                reduce(NI, 0, TAIL)
                count(NI, 0, TAIL)
                v.wait_ge(pe_done, 1)
                step(v.tensor_copy(r.deg[:, :], cnt_ps[:, 0:NB]))
                step(v.tensor_copy(r.pos_i, r.pos))
                step(v.tensor_scalar(keyi, r.pos_i, P - 1, None, ALU.bitwise_and))
                step(v.tensor_scalar(r.pos_i, r.pos_i, 7, None, ALU.arith_shift_right))
                step(v.scalar_tensor_tensor(r.pos_i, keyi, float(XR), r.pos_i, ALU.mult, ALU.add))

        if first:
            @block.scalar
            def _(act):
                def keep(i, s, nb):
                    act.wait_ge(gathered[s], (i + 1) * (16 * B) if nb == B else NI * 16 * B + 16 * nb)
                    act.wait_ge(kept[s], i * 16 + 16)
                    act.activation(emb[:, s, 0:nb, :], ring[:, s, 0:nb, H:], ACT.Copy).then_inc(emb_ready, 1)
                act.wait_ge(zero_ready, 2)
                with act.Fori(0, NI) as i:
                    for s in range(2):
                        keep(i, s, B)
                        for array, width in ((d.spread, WX), (d.records, WR)):
                            part = ZR // 2 * width
                            act.dma_start(array.rearrange("(p j) c -> p (j c)", p=P)[:, bass.ds((i * 2 + s) * part, part)],
                                          zero[:, 0:part]).then_inc(zeroed, 16)
                keep(NI, 0, TAIL)
                act.wait_ge(zeroed, 64 * NI)

            @block.tensor
            def _(pe):
                pe.wait_ge(zero_ready, 2)
                pe.matmul(cnt_ps[:, 0:NB], lhsT=zb[:, :], rhs=zb[:, 0:NB], start=True, stop=False, skip_group_check=True)

                def columns(i, s, half, nb):
                    pe.wait_ge(hot_ready, i * 4 + (2 * s + half + 1))
                    for b in range(nb):
                        last = pe.matmul(cnt_ps[:, 0:NB], lhsT=hot[:, half, b, 0:P], rhs=hot[:, half, b, P:], start=False, stop=False,
                                         skip_group_check=True)
                    last.then_inc(hot_used, 1)

                def turns(lo, hi):
                    with pe.Fori(lo, hi) as i:
                        for s in range(2):
                            for half in range(2):
                                columns(i, s, half, HB)
                turns(0, TA)
                pe.wait_ge(counted, 1)
                pe.matmul(base_ps[:, 0, 0:P], lhsT=r.ones[:, :], rhs=cnt[:, :], start=True, stop=True)
                pe.matmul(base_ps[:, 1, 0:P], lhsT=r.before[:, :], rhs=cnt[:, :], start=True, stop=True).then_inc(base_made, 1)
                turns(TA, NI)
                columns(NI, 0, 0, TAIL)
                pe.matmul(cnt_ps[:, 0:NB], lhsT=zb[:, :], rhs=zb[:, 0:NB], start=False, stop=True, skip_group_check=True).then_inc(pe_done, 1)


def mend_and_take(nc, c, sem, name, state_dram, largest, ends, out):
    d, r = c.d, c.r
    with ExitStack() as ctx:
        sb = lambda n, s, t=F32: ctx.enter_context(nc.sbuf_tensor(name + n, s, t))
        last, lastT, flagT, carry, carried, row = (sb("last", [P, H]), sb("lastT", [H, P]), sb("flagT", [H, P]), sb("carry", [H, P + 1]),
                                                   sb("carried", [P, H]), sb("row", [P, H]))
        tps = ctx.enter_context(nc.psum_tensor(name + "t", [P, 512], F32))
        t2s = ctx.enter_context(nc.psum_tensor(name + "t2", [P, 512], F32))
        ld, rd, dv, pt, mended, taken, started, stored = (sem(f"{name}_{n}") for n in ("last", "row", "dve", "pe", "mended", "taken", "started", "stored"))
        block = ctx.enter_context(nc.Block())

        @block.sync
        def _(sp):
            sp.dma_start(last[:, :], state_dram[0:E, :].rearrange("(p j) c -> p j c", p=P)[:, J - 1, :]).then_inc(ld, 16)
            sp.wait_ge(ld, 16)

        @block.tensor
        def _(pe):
            pe.wait_ge(ld, 16)
            pe.transpose(tps[0:H, 0:P], last[:, :], r.ident[:, :]).then_inc(pt, 1)
            pe.wait_ge(started, 1)
            pe.transpose(t2s[:, 0:H], carry[:, 0:P], r.ident[0:H, 0:H]).then_inc(pt, 1)

        @block.vector
        def _(v):
            step = Steps(v, dv)
            if largest:
                step(v.tensor_scalar(flagT[:, :], r.full[:, :], 2.0, -1.0, ALU.mult, ALU.add))
                step(v.tensor_scalar(flagT[:, :], flagT[:, :], FMAX, None, ALU.mult))
            else:
                step(v.tensor_copy(flagT[:, :], r.full[:, :]))
            neutral = -FMAX if largest else 0.0
            step(v.memset(carry[:, 0:1], neutral))
            v.wait_ge(pt, 1)
            step(v.tensor_copy(lastT[:, :], tps[0:H, 0:P]))
            step(v.tensor_tensor_scan(carry[:, 1:], flagT[:, :], lastT[:, :], neutral, ALU.min if largest else ALU.mult, ALU.max if largest else ALU.add))
            v.sem_inc(started, 1)
            v.wait_ge(pt, 2)
            step(v.tensor_copy(carried[:, :], t2s[:, 0:H]))
            v.wait_ge(rd, 16)
            step(v.tensor_tensor(row[:, :], row[:, :], carried[:, :], ALU.max if largest else ALU.add))
            v.sem_inc(mended, 1)

        @block.gpsimd
        def _(gp):
            gp.indirect_dma_start(row[:, :], None, state_dram, bass.IndirectOffsetOnAxis(ap=r.mend_read[:, :], axis=0)).then_inc(rd, 16)
            gp.wait_ge(mended, 1)
            gp.indirect_dma_start(state_dram, bass.IndirectOffsetOnAxis(ap=r.mend_write[:, :], axis=0), row[:, :], None).then_inc(stored, 16)
            gp.wait_ge(stored, 16)
            for b in range(NB):
                gp.indirect_dma_start(out[:, b, :], None, state_dram, bass.IndirectOffsetOnAxis(ap=ends[:, b:b + 1], axis=0)).then_inc(taken, 16)
            gp.wait_ge(taken, 16 * NB)


def rows_of_dst(nc, c, sem):
    r = c.r
    with (
        nc.sbuf_tensor("rd_a", [P, 5, NB], F32) as w,
        nc.sbuf_tensor("rd_node", [P, NB], I32) as node,
        nc.psum_tensor("rd_ps", [P, 2, 256], F32) as ps,
        nc.Block() as block,
    ):
        pt, dv, it = sem("rd_pe"), sem("rd_dve"), sem("rd_iota")

        @block.gpsimd
        def _(gp):
            gp.iota(node[:, :], pattern=[[P, NB]], base=E, channel_multiplier=1).then_inc(it, 1)

        @block.tensor
        def _(pe):
            pe.matmul(ps[:, 0, 0:NB], lhsT=r.before[:, :], rhs=r.deg[:, :], start=True, stop=True)
            pe.matmul(ps[:, 1, 0:NB], lhsT=r.ones[:, :], rhs=r.deg[:, :], start=True, stop=True).then_inc(pt, 1)

        @block.vector
        def _(v):
            step = Steps(v, dv)
            v.wait_ge(pt, 1)
            step(v.tensor_copy(w[:, 0, :], ps[:, 1, 0:NB]))
            step(v.tensor_tensor_scan(w[:, 1, :], w[:, 0, :], w[:, 0, :], 0.0, ALU.add, ALU.bypass))
            step(v.tensor_tensor(w[:, 1, :], w[:, 1, :], w[:, 0, :], ALU.subtract))
            step(v.tensor_tensor(w[:, 1, :], w[:, 1, :], ps[:, 0, 0:NB], ALU.add))
            step(v.scalar_tensor_tensor(w[:, 2, :], w[:, 1, :], -1.0, r.deg[:, :], ALU.add, ALU.add))
            step(v.tensor_scalar(r.ends[:, :], w[:, 2, :], 0.0, None, ALU.max))
            v.wait_ge(it, 1)
            step(v.tensor_tensor(w[:, 3, :], node[:, :], w[:, 1, :], ALU.subtract))
            step(v.scalar_tensor_tensor(w[:, 3, :], r.deg[:, :], 0.0, w[:, 3, :], ALU.is_equal, ALU.mult))
            step(v.tensor_tensor(r.starts[:, :], w[:, 3, :], w[:, 1, :], ALU.add))


def layer0_finish(nc, c, sem):
    d, r = c.d, c.r
    with ExitStack() as ctx:
        took = ctx.enter_context(nc.sbuf_tensor("took0", [P, NB, H], F32))
        mend_and_take(nc, c, sem, "m0", d.state, True, r.ends, took)
        stat = ctx.enter_context(nc.sbuf_tensor("stat1", [P, 4, NB], F32))
        rows = ctx.enter_context(nc.sbuf_tensor("rows1", [P, NB, WX], F32))
        block = ctx.enter_context(nc.Block())
        dv, ready, rt, rows_ready, wr, angle, sine = (sem("f0_" + n) for n in ("dve", "var", "root", "rows", "written", "angle", "sine"))

        @block.vector
        def _(v):
            step = Steps(v, dv)
            step(v.tensor_tensor(r.a[:, :, :], r.a[:, :, :], took[:, :, :], ALU.add))
            step(v.tensor_scalar(stat[:, 0, :], r.deg[:, :], 0.0, None, ALU.is_gt))
            step(v.tensor_tensor(r.a[:, :, :], r.a[:, :, :], bc(stat[:, 0, :].unsqueeze(2), 2, H), ALU.mult))
            step(v.tensor_tensor(r.x[:, :, :], r.x[:, :, :], r.a[:, :, :], ALU.add))
            step(v.tensor_copy(rows[:, :, H], r.mult[:, :]))
            step(v.tensor_copy(rows[:, :, H + 1:], r.e2[:, :, :]))
            layernorm_relu(nc, v, step, (rt, 1), ready, r.a[:, :, :], r.x[:, :, :], took[:, :, :], stat)
            step(v.tensor_copy(rows[:, :, 0:H], r.a[:, :, :]))
            v.sem_inc(rows_ready, 1)
            cut = r.cut
            step(v.scalar_tensor_tensor(cut, r.w, -1.0, r.w, ALU.mult, ALU.max))
            step(v.tensor_scalar(cut, cut, 6.0, -PI / 6.0, ALU.min, ALU.mult))
            step(v.tensor_scalar(cut, cut, PI / 2.0, None, ALU.add))
            v.sem_inc(angle, 1)
            v.wait_ge(sine, 1)
            step(v.tensor_scalar(cut, cut, 0.5, 0.5, ALU.mult, ALU.add))
            step(v.scalar_tensor_tensor(cut, r.w, 6.0, cut, ALU.is_lt, ALU.mult))

        @block.scalar
        def _(act):
            root(nc, act, ready, 1, rt, stat)
            act.wait_ge(angle, 1)
            act.activation(r.cut, r.cut, ACT.Sin).then_inc(sine, 1)

        @block.sync
        def _(sp):
            sp.wait_ge(rows_ready, 1)
            sp.dma_start(nodes(d.rows1), rows[:, :, :]).then_inc(wr, 16)
            sp.wait_ge(wr, 16)

        @block.gpsimd
        def _(gp):
            gp.wait_ge(rows_ready, 1)
            sc = sem("f0_scattered")
            for b in range(NB):
                gp.indirect_dma_start(d.spread, bass.IndirectOffsetOnAxis(ap=r.starts[:, b:b + 1], axis=0), rows[:, b, :], None).then_inc(sc, 16)
            gp.wait_ge(sc, 16 * NB)


def store_x(nc, c, sem):
    d, r = c.d, c.r
    done = sem("out_stored")
    with nc.Block() as block:
        @block.sync
        def _(sp):
            sp.dma_start(nodes(d.out[0:(NB - 1) * P, :]), r.x[:, 0:NB - 1, :]).then_inc(done, 16)
            sp.dma_start(d.out[(NB - 1) * P:N, :], r.x[0:LAST, NB - 1, :]).then_inc(done, 16)
            sp.wait_ge(done, 32)


def layer1_edges(nc, c, sem):
    d, r = c.d, c.r
    SB = 8
    KB = B // SB
    with ExitStack() as ctx:
        sb = lambda n, s, t=F32: ctx.enter_context(nc.sbuf_tensor("e1" + n, s, t))
        spread, attr, emb = sb("spread", [P, 2, B, WX]), sb("attr", [P, 2, B, A]), sb("emb", [P, 2, B, EM])
        row = sb("row", [P, 2, B, WX])
        same = sb("same", [P, 2, B])
        prod, logit, coef, gate, lo = sb("prod", [P, B, EM]), sb("logit", [P, B]), sb("coef", [P, B]), sb("gate", [P, SB, H]), sb("lo", [P, B], I32)
        rec, slot = sb("rec", [P, 2, B, WR]), sb("slot", [P, 2, B], I32)
        w1, w2, b1 = sb("w1", [2 * A, 2 * H]), sb("w2", [2 * H + 1, 2 * H]), sb("b1", [2 * H, 1])
        attrT, hidden = sb("attrT", [2 * A, 2, SB // 2 * P]), sb("hidden", [2 * H + 1, 2, SB // 2 * P])
        ps = lambda n: [ctx.enter_context(nc.psum_tensor(f"e1{n}{s}", [P, 512], F32)) for s in range(2)]
        tp, hp, gp_ps = ps("tp"), ps("hp"), ps("gp")
        two = lambda n: [sem(f"e1_{n}{s}") for s in range(2)]
        spread_in, attr_in, emb_in, scattered = two("spread_in"), two("attr_in"), two("emb_in"), two("scattered")
        (w_in, cleared, first_row, spread_used, emb_used, turned, turned_back, hid, act_done, gated, gate_used, rec_ready, pool_go,
         dv, dv0) = (sem("e1_" + n) for n in ("w_in", "cleared", "first_row", "spread_used", "emb_used", "turned", "turned_back",
                                              "hid", "act_done", "gated", "gate_used", "rec_ready", "pool_go", "dve", "dve0"))
        block = ctx.enter_context(nc.Block())

        @block.sync
        def _(sp):
            spread_v = d.spread[0:E, :].rearrange("(p j) c -> p j c", p=P)
            attr_v = d.attr.rearrange("(p j) c -> p j c", p=P)
            emb_v = d.emb_edge.rearrange("(p j) c -> p j c", p=P)
            sp.wait_ge(cleared, 2)
            for k in range(2):
                sp.dma_start(w1[k * A:(k + 1) * A, k * H:(k + 1) * H], d.W1.rearrange("o i -> i o")).then_inc(w_in, 16)
                sp.dma_start(w2[k * H:(k + 1) * H, k * H:(k + 1) * H], d.W2.rearrange("o i -> i o")).then_inc(w_in, 16)
                sp.dma_start(w2[2 * H:2 * H + 1, k * H:(k + 1) * H], d.b2.rearrange("(o f) -> o f", o=1)).then_inc(w_in, 16)
                sp.dma_start(b1[k * H:(k + 1) * H, :], d.b1.rearrange("(f o) -> f o", o=1)).then_inc(w_in, 16)

            def load(g, s, nb):
                sp.wait_ge(turned, g * KB + 1)
                sp.dma_start(attr[:, s, 0:nb, :], attr_v[:, bass.ds(g * B, nb), :]).then_inc(attr_in[s], 16)
                sp.wait_ge(spread_used, g + 1)
                sp.dma_start(spread[:, s, 0:nb, :], spread_v[:, bass.ds(g * B, nb), :]).then_inc(spread_in[s], 16)
                sp.wait_ge(emb_used, g + 1)
                sp.dma_start(emb[:, s, 0:nb, :], emb_v[:, bass.ds(g * B, nb), :]).then_inc(emb_in[s], 16)
            with sp.Fori(0, NI) as i:
                for s in range(2):
                    load(i * 2 + s, s, B)
            load(2 * NI, 0, TAIL)
            for s in range(2):
                for q in (attr_in, spread_in, emb_in):
                    sp.wait_ge(q[s], 16 * (NI + 1 - s))
            sp.wait_ge(w_in, 128)

        @block.tensor
        def _(pe):
            pe.sem_inc(hid, 2)
            pe.sem_inc(gated, 2)
            pe.sem_inc(turned, KB + 1)
            pe.wait_ge(w_in, 128)
            pe.wait_ge(cleared, 3)

            def group(i, s, nb):
                pe.wait_ge(attr_in[s], i * 16 + 16)
                for k in range(-(-nb // SB)):
                    u, q = i * (2 * KB) + (s * KB + k), (s * KB + k) % 2
                    pairs = min(SB // 2, -(-(nb - k * SB) // 2))
                    pe.wait_ge(turned_back, u + 1)
                    for m in range(pairs):
                        b = k * SB + 2 * m
                        last = pe.transpose(tp[q][0:2 * A, m * P:(m + 1) * P], attr[:, s, b:b + 2, :].rearrange("p b a -> p (b a)"), r.ident[:, :])
                    last.then_inc(turned, 1)
                    pe.wait_ge(turned_back, u + 3)
                    pe.wait_ge(act_done, u + 1)
                    pe.matmul(hp[q][0:2 * H, 0:pairs * P], lhsT=w1[:, :], rhs=attrT[:, q, 0:pairs * P], start=True, stop=True).then_inc(hid, 1)
                    pe.wait_ge(act_done, u + 3)
                    pe.wait_ge(gate_used, u + 1)
                    for m in range(pairs):
                        last = pe.matmul(gp_ps[q][:, m * 2 * H:(m + 1) * 2 * H], lhsT=hidden[:, q, m * P:(m + 1) * P], rhs=w2[:, :],
                                         start=True, stop=True)
                    last.then_inc(gated, 1)
            with pe.Fori(0, NI) as i:
                for s in range(2):
                    group(i, s, B)
            group(NI, 0, TAIL)

        @block.scalar
        def _(act):
            act.sem_inc(turned_back, 2)
            act.sem_inc(act_done, 2)
            act.wait_ge(w_in, 128)

            def group(i, s, nb):
                for k in range(-(-nb // SB)):
                    u, q = i * (2 * KB) + (s * KB + k), (s * KB + k) % 2
                    n = min(SB // 2, -(-(nb - k * SB) // 2)) * P
                    act.wait_ge(hid, u + 1)
                    act.wait_ge(turned, u + KB + 2)
                    act.activation(attrT[:, q, 0:n], tp[q][0:2 * A, 0:n], ACT.Copy).then_inc(turned_back, 1)
                    act.wait_ge(gated, u + 1)
                    act.wait_ge(hid, u + 3)
                    act.activation(hidden[0:2 * H, q, 0:n], hp[q][0:2 * H, 0:n], ACT.Silu, bias=b1[:, :]).then_inc(act_done, 1)
            with act.Fori(0, NI) as i:
                for s in range(2):
                    group(i, s, B)
            group(NI, 0, TAIL)

        @block.gpsimd
        def _(gp):
            gp.indirect_dma_start(row[:, 1, B - 1, :], None, d.rows1, bass.IndirectOffsetOnAxis(ap=r.first_dst[:, :], axis=0)).then_inc(first_row, 16)

            def scatter(s, nb):
                for b in range(nb):
                    gp.indirect_dma_start(d.records, bass.IndirectOffsetOnAxis(ap=slot[:, s, b:b + 1], axis=0), rec[:, s, b, :], None).then_inc(scattered[s], 16)
            with gp.Fori(0, NI) as i:
                for s in range(2):
                    gp.wait_ge(rec_ready, i * 2 + (s + 1))
                    gp.sem_inc(pool_go, 1)
                    scatter(s, B)
            gp.wait_ge(rec_ready, 2 * NI + 1)
            scatter(0, TAIL)
            gp.wait_ge(scattered[0], 16 * (NI * B + TAIL))
            gp.wait_ge(scattered[1], 16 * NI * B)

        @block.vector
        def _(v):
            step = Steps(v, dv)
            v.memset(w1[:, :], 0.0).then_inc(cleared, 1)
            v.memset(w2[:, :], 0.0).then_inc(cleared, 1)
            v.memset(hidden[2 * H:2 * H + 1, :, :], 1.0).then_inc(cleared, 1)
            v.sem_inc(spread_used, 2)
            v.sem_inc(emb_used, 2)
            v.sem_inc(gate_used, 2)
            v.wait_ge(first_row, 16)

            def group(i, s, nb, first=False):
                g = i * 2 + s
                cols = bass.ds(g * B, nb)
                step(v.tensor_scalar(same[:, s, 0:nb], r.same[:, cols], 1.0, None, ALU.mult))
                v.wait_ge(spread_in[s], i * 16 + 16)
                for b in range(nb):
                    prev = row[:, s, b - 1, :] if b else row[:, 1 - s, B - 1, :]
                    step(v.scalar_tensor_tensor(row[:, s, b, :], prev, same[:, s, b:b + 1], spread[:, s, b, :], ALU.mult, ALU.add))
                v.sem_inc(spread_used, 1)
                v.wait_ge(emb_in[s], i * 16 + 16)
                step(v.tensor_tensor(prod[:, 0:nb, :], emb[:, s, 0:nb, :], row[:, s, 0:nb, H + 1:], ALU.mult))
                v.sem_inc(emb_used, 1)
                step(v.tensor_reduce(logit[:, 0:nb], prod[:, 0:nb, :], AX, ALU.add))
                step(v.tensor_tensor(coef[:, 0:nb], r.cut[:, cols], row[:, s, 0:nb, H], ALU.mult))
                if not first:
                    v.wait_ge(scattered[s], i * (16 * B))
                step(v.tensor_scalar(rec[:, s, 0:nb, H], row[:, s, 0:nb, H], 1.0, None, ALU.mult))
                step(v.tensor_scalar(rec[:, s, 0:nb, H + 1], r.w[:, cols], 1.0, None, ALU.mult))
                step(v.tensor_scalar(rec[:, s, 0:nb, H + 2], r.gidx[:, cols], 1.0, None, ALU.mult))
                step(v.tensor_scalar(lo[:, 0:nb], r.src[:, cols], P - 1, None, ALU.bitwise_and))
                step(v.tensor_scalar(rec[:, s, 0:nb, H + 3], lo[:, 0:nb], 1.0, None, ALU.mult))
                step(v.tensor_scalar(slot[:, s, 0:nb], r.pos_i[:, cols], 0.0, None, ALU.add))
                for k in range(-(-nb // SB)):
                    u, q = i * (2 * KB) + (s * KB + k), (s * KB + k) % 2
                    n, b = min(SB, nb - k * SB), k * SB
                    v.wait_ge(gated, u + 3)
                    ins = v.tensor_tensor(gate[:, 0:n, :], gp_ps[q][:, 0:n * H].rearrange("p (b f) -> p b f", f=H),
                                          bc(logit[:, b:b + n].unsqueeze(2), 2, H), ALU.add)
                    step(ins)
                    v.sem_inc(gate_used, 1)
                    step(v.tensor_tensor(gate[:, 0:n, :], gate[:, 0:n, :], row[:, s, b:b + n, 0:H], ALU.mult))
                    step(v.tensor_tensor(rec[:, s, b:b + n, 0:H], gate[:, 0:n, :], bc(coef[:, b:b + n].unsqueeze(2), 2, H), ALU.mult))
                v.sem_inc(rec_ready, 1)
            for s in range(2):
                group(0, s, B, first=True)
            with v.Fori(1, NI) as i:
                step.enter(i - 1, 2 * (1 + B + 3 + 6 + 3 * KB))
                for s in range(2):
                    group(i, s, B)
            step.leave(NI - 1)
            group(NI, 0, TAIL)


def tile_blocks(nc, c, sem):
    r = c.r
    W = 496
    assert r.offset.shape[1] % W == 0
    with (
        nc.sbuf_tensor("tb_tile", [P, T // 13 * 16], I32) as tile,
        nc.sbuf_tensor("tb_ge", [P, T // 13 * 16], F32) as ge,
        nc.sbuf_tensor("tb_first", [P, P], F32) as first,
        nc.psum_tensor("tb_ft", [P, 512], F32) as ft,
        nc.psum_tensor("tb_n", [P, 2, 512], F32) as cnt,
        nc.Block() as block,
    ):
        it, pt, dv = sem("tb_iota"), sem("tb_pe"), sem("tb_dve")

        @block.gpsimd
        def _(gp):
            gp.iota(tile[:, :], pattern=[[13, T // 13], [1, 16]], base=0, channel_multiplier=0).then_inc(it, 1)

        @block.tensor
        def _(pe):
            pe.transpose(ft[:, 0:P], r.first_tile[:, :], r.ident[:, :]).then_inc(pt, 1)
            for k in range(r.offset.shape[1] // W):
                pe.wait_ge(dv, 2 if k < 2 else k + 1)
                pe.matmul(cnt[0:1, k % 2, 0:W], lhsT=r.ones[0:NB, 0:1], rhs=ge[0:NB, k * W:(k + 1) * W], start=True, stop=True).then_inc(pt, 1)

        @block.vector
        def _(v):
            step = Steps(v, dv)
            v.wait_ge(pt, 1)
            step(v.tensor_copy(first[:, :], ft[:, 0:P]))
            v.wait_ge(it, 1)
            step(v.tensor_scalar(ge[:, :], tile[:, :], first[:, 0:1], None, ALU.is_ge))
            for k in range(r.offset.shape[1] // W):
                v.wait_ge(pt, k + 2)
                step(v.tensor_scalar(r.offset[0:1, k * W:(k + 1) * W], cnt[0:1, k % 2, 0:W], -1.0, float(H + 1), ALU.add, ALU.mult))


def load_offsets(nc, v, offset, g, half):
    _, vals = nc.values_load_multi_w_load_instructions(
        offset[0:1, bass.ds(g * 32 + half * 16, 13)], engines=[v.engine], min_val=0, max_val=(NB - 1) * (H + 1),
        skip_runtime_bounds_check_because="a block's number times a row's width, from tile_blocks")
    return vals


def sum_by_src(nc, c, sem, name, table, acc, width):
    d, r = c.d, c.r
    lay1 = table is None
    GT = T // BT
    with ExitStack() as ctx:
        sb = lambda n, s, t=F32: ctx.enter_context(nc.sbuf_tensor(name + n, s, t))
        ring = sb("ring", [P, 2, BT, WR if lay1 else H])
        hot = sb("hot", [P, 2, BT, P])
        banks = [[ctx.enter_context(nc.psum_tensor(f"{name}ps{s}{k}", [P, 512], F32)) for k in range(3)] for s in range(2)]
        landed = [sem(f"{name}_landed{s}") for s in range(2)]
        free, hot_ready, summed, kept, go, dv, idx_ready, pe_go = (sem(f"{name}_{n}") for n in ("free", "hot_ready", "summed", "kept", "go", "dve", "idx_ready", "pe_go"))
        if not lay1:
            idx, small = sb("idx", [P, 2, BT], I32), sb("small", [P, 2, BT])
        block = ctx.enter_context(nc.Block())

        if lay1:
            @block.sync
            def _(sp):
                rec_v = d.records.rearrange("(p j) c -> p j c", p=P)

                def load(g, s):
                    sp.wait_ge(summed, g + 1)
                    sp.wait_ge(kept, g + 1)
                    sp.dma_start(ring[:, s, :, :], rec_v[:, bass.ds(g * BT, BT), :]).then_inc(landed[s], 16)
                with sp.Fori(0, NT) as i:
                    for s in range(2):
                        load(i * 2 + s, s)
                load(GT, 0)
                sp.wait_ge(landed[0], 16 * (NT + 1))
                sp.wait_ge(landed[1], 16 * NT)

            @block.scalar
            def _(act):
                act.sem_inc(kept, 2)
                with act.Fori(0, NT) as i:
                    for s in range(2):
                        act.wait_ge(landed[s], i * 16 + 16)
                        act.sem_inc(go, 1)
                        cols = bass.ds((i * 2 + s) * BT, BT)
                        act.activation(r.w3[:, cols], ring[:, s, :, H + 1], ACT.Copy)
                        act.activation(r.row3[:, cols], ring[:, s, :, H + 2], ACT.Copy)
                        act.activation(r.lo3[:, cols], ring[:, s, :, H + 3], ACT.Copy).then_inc(kept, 1)
        else:
            @block.gpsimd
            def _(gp):
                with gp.Fori(0, NT) as i:
                    for s in range(2):
                        gp.wait_ge(idx_ready, i * 2 + (s + 1))
                        gp.sem_inc(go, 1)
                        for b in range(BT):
                            gp.indirect_dma_start(ring[:, s, b, :], None, table,
                                                  bass.IndirectOffsetOnAxis(ap=idx[:, s, b:b + 1], axis=0)).then_inc(landed[s], 16)

        @block.tensor
        def _(pe):
            pe.sem_inc(summed, 2)
            with pe.Fori(0, NT) as i:
                for s in range(2):
                    g = i * 2 + s
                    pe.wait_ge(landed[s], (i + 1) * (16 if lay1 else 16 * BT))
                    pe.wait_ge(hot_ready, g + 1)
                    pe.wait_ge(free, g + 1)
                    for b in range(BT):
                        last = pe.matmul(banks[s][b // 10][:, b % 10 * width:(b % 10 + 1) * width], lhsT=hot[:, s, b, :], rhs=ring[:, s, b, 0:width],
                                         start=True, stop=True)
                    last.then_inc(summed, 1)

        @block.vector
        def _(v):
            step = Steps(v, dv)
            v.sem_inc(free, 2)

            def onehots(i, g, s):
                if lay1:
                    v.wait_ge(landed[s], i * 16 + 16)
                    v.tensor_tensor(hot[:, s, :, :], bc(r.iota[:, :].unsqueeze(1), 1, BT), bc(ring[:, s, :, H + 3:H + 4], 2, P),
                                    ALU.is_equal).then_inc(hot_ready, 1)
                else:
                    step(v.tensor_scalar(small[:, 0, :], r.lo3[:, bass.ds(g * BT, BT)], 1.0, None, ALU.mult))
                    step(v.tensor_scalar(small[:, 1, :], r.w3[:, bass.ds(g * BT, BT)], 1.0, None, ALU.mult))
                    for b in range(BT):
                        ins = v.tensor_scalar(hot[:, s, b, :], r.iota[:, :], small[:, 0, b:b + 1], small[:, 1, b:b + 1], ALU.is_equal, ALU.mult)
                    step(ins)
                    v.sem_inc(hot_ready, 1)

            def stage(g, s):
                v.tensor_scalar(idx[:, s, :], r.row3[:, bass.ds(g * BT, BT)], 0.0, None, ALU.add).then_inc(idx_ready, 1)

            step(v.memset(acc[:, :, :], 0.0))
            flat = acc[:, :, :].rearrange("p b f -> p (b f)")
            if not lay1:
                for q in (r.w3, r.lo3):
                    step(v.memset(q[:, T:], 0.0))
                step(v.memset(r.row3[:, T:], 0))
                for s in range(2):
                    stage(s, s)
            onehots(0, 0, 0)
            with v.Fori(0, NT) as i:
                step.enter(i, 2 * BT + (0 if lay1 else 6))
                for s in range(2):
                    g = i * 2 + s
                    onehots(i + s, g + 1, 1 - s)
                    for half in range(2):
                        offs = load_offsets(nc, v, r.offset, g, half)
                        if half == 0:
                            v.wait_ge(summed, g + 3)
                        for k in range(13):
                            b = half * 13 + k
                            part = flat[:, bass.ds(offs[k], width)]
                            step(v.tensor_tensor(part, part, banks[s][b // 10][:, b % 10 * width:(b % 10 + 1) * width], ALU.add))
                    v.sem_inc(free, 1)
                    if not lay1:
                        stage(g + 2, s)
            step.leave(NT)


def layer1_finish(nc, c, sem, acc):
    d, r = c.d, c.r
    with ExitStack() as ctx:
        sb = lambda n, s, t=F32: ctx.enter_context(nc.sbuf_tensor("f1" + n, s, t))
        stat, y, vec, w = sb("stat", [P, 4, NB]), sb("y", [P, NB, H]), sb("vec", [P, 2, H]), sb("w", [H, H])
        tmp = acc[:, :, 0:H]
        ld, dv, ready, rt, done, wr = (sem("f1_" + n) for n in ("w_in", "dve", "var", "root", "done", "written"))
        prod = NodeProduct(nc, ctx, sem, "n2", w[:, :], H)
        block = ctx.enter_context(nc.Block())

        @block.sync
        def _(sp):
            sp.dma_start(vec[:, 0, :], bcast_row(d.gamma)).then_inc(ld, 16)
            sp.dma_start(vec[:, 1, :], bcast_row(d.beta)).then_inc(ld, 16)
            sp.dma_start(w[:, :], d.W_2).then_inc(ld, 16)
            sp.wait_ge(ld, 48)
            sp.wait_ge(done, 1)
            sp.dma_start(nodes(d.rows2), r.a[:, :, :]).then_inc(wr, 16)
            sp.wait_ge(wr, 16)

        @block.vector
        def _(v):
            step = Steps(v, dv)
            step(v.tensor_scalar(stat[:, 0, :], acc[:, :, H], 1e-8, None, ALU.max))
            step(v.reciprocal(stat[:, 0, :], stat[:, 0, :]))
            step(v.tensor_tensor(y[:, :, :], acc[:, :, 0:H], bc(stat[:, 0, :].unsqueeze(2), 2, H), ALU.mult))
            step(v.tensor_tensor(r.a[:, :, :], r.a[:, :, :], y[:, :, :], ALU.add))
            layernorm_relu(nc, v, step, (rt, 1), ready, y[:, :, :], r.a[:, :, :], tmp, stat, relu=False)
            v.wait_ge(ld, 48)
            step(v.tensor_tensor(y[:, :, :], y[:, :, :], bc(vec[:, 0:1, :], 1, NB), ALU.mult))
            step(v.tensor_tensor(y[:, :, :], y[:, :, :], bc(vec[:, 1:2, :], 1, NB), ALU.add))
            step(v.tensor_tensor(r.x[:, :, :], r.x[:, :, :], y[:, :, :], ALU.add))
            step(v.tensor_scalar(stat[:, 1, :], r.deg[:, :], 1.0, None, ALU.add))
            v.sem_inc(ready, 1)
            v.wait_ge(rt, 2)
            step(v.reciprocal(r.dinv[:, :], stat[:, 2, :]))
            layernorm_relu(nc, v, step, (rt, 3), ready, r.a[:, :, :], r.x[:, :, :], tmp, stat)

            def take(g, s, nb, rows):
                return v.tensor_tensor(r.a[:, bass.ds(g * prod.CB, nb), :], rows[0], bc(r.dinv[:, bass.ds(g * prod.CB, nb)].unsqueeze(2), 2, H), ALU.mult)
            prod.on_vector(v, r.a, take)
            v.sem_inc(done, 1)

        @block.scalar
        def _(act):
            for k in range(3):
                root(nc, act, ready, k + 1, rt, stat)
            prod.on_scalar(act)

        @block.tensor
        def _(pe):
            pe.wait_ge(ld, 48)
            prod.on_tensor(pe, r.ident)


def layer2_finish(nc, c, sem):
    d, r = c.d, c.r
    with ExitStack() as ctx:
        sb = lambda n, s, t=F32: ctx.enter_context(nc.sbuf_tensor("f2" + n, s, t))
        took = sb("took", [P, NB, H])
        mend_and_take(nc, c, sem, "m2", d.state2, False, r.ends, took)
        stat, b, w = sb("stat", [P, 4, NB]), sb("b", [P, 1, H]), sb("w", [H, NR * H])
        y = sb("y", [P, 2, NodeProduct.CB, NR * H])
        ld, dv, ready, rt = (sem("f2_" + n) for n in ("w_in", "dve", "var", "root"))
        wr = [sem(f"f2_written{s}") for s in range(2)]
        prod = NodeProduct(nc, ctx, sem, "n3", w[:, :], NR * H)
        block = ctx.enter_context(nc.Block())

        @block.sync
        def _(sp):
            sp.dma_start(w[:, :].rearrange("i (r o) -> i r o", r=NR), d.W_3.rearrange("(r i) o -> i r o", r=NR)).then_inc(ld, 16)
            sp.dma_start(b[:, 0, :], bcast_row(d.b_2)).then_inc(ld, 16)
            sp.wait_ge(ld, 32)
            rows_v = d.rows3.rearrange("(b p r) c -> p b (r c)", p=P, r=NR)
            for s in range(2):
                sp.sem_inc(wr[s], 16)

            def chunk(g, s, nb):
                sp.wait_ge(prod.taken, g + 1)
                sp.dma_start(rows_v[:, bass.ds(g * prod.CB, nb), :], y[:, s, 0:nb, :]).then_inc(wr[s], 16)
            prod.chunks(sp, chunk)
            sp.wait_ge(wr[0], 16 * (prod.TURNS + 2))
            sp.wait_ge(wr[1], 16 * (prod.TURNS + 1))

        @block.vector
        def _(v):
            step = Steps(v, dv)
            has = stat[:, 0, :]
            step(v.tensor_scalar(has, r.deg[:, :], 0.0, None, ALU.is_gt))
            step(v.tensor_tensor(took[:, :, :], took[:, :, :], bc(has.unsqueeze(2), 2, H), ALU.mult))
            step(v.tensor_tensor(r.a[:, :, :], r.a[:, :, :], took[:, :, :], ALU.add))
            step(v.tensor_tensor(r.a[:, :, :], r.a[:, :, :], bc(r.dinv[:, :].unsqueeze(2), 2, H), ALU.mult))
            v.wait_ge(ld, 32)
            step(v.tensor_tensor(r.a[:, :, :], r.a[:, :, :], bc(b[:, :, :], 1, NB), ALU.add))
            step(v.tensor_tensor(r.x[:, :, :], r.x[:, :, :], r.a[:, :, :], ALU.add))
            layernorm_relu(nc, v, step, (rt, 1), ready, r.a[:, :, :], r.x[:, :, :], took[:, :, :], stat)

            def take(g, s, nb, rows):
                v.wait_ge(wr[s], (g - s) * 8 + 16)
                for k, part in enumerate(rows):
                    n = part.shape[1]
                    last = v.tensor_copy(y[:, s, k * prod.per:k * prod.per + n, :], part)
                return last
            prod.on_vector(v, r.a, take)

        @block.scalar
        def _(act):
            root(nc, act, ready, 1, rt, stat)
            prod.on_scalar(act)

        @block.tensor
        def _(pe):
            pe.wait_ge(ld, 32)
            prod.on_tensor(pe, r.ident)


def layer3_finish(nc, c, sem, acc):
    d, r = c.d, c.r
    ld, dv = sem("f3_b_in"), sem("f3_dve")
    with nc.sbuf_tensor("f3b", [P, 1, H], F32) as b, nc.Block() as block:
        @block.sync
        def _(sp):
            sp.dma_start(b[:, 0, :], bcast_row(d.b_3)).then_inc(ld, 16)
            sp.wait_ge(ld, 16)

        @block.vector
        def _(v):
            step = Steps(v, dv)
            step(v.tensor_tensor(r.x[:, :, :], r.x[:, :, :], acc[:, :, 0:H], ALU.add))
            v.wait_ge(ld, 16)
            step(v.tensor_tensor(r.x[:, :, :], r.x[:, :, :], bc(b[:, :, :], 1, NB), ALU.add))


def gnn(nc, x, src, dst, edge_attr_40, edge_type_4, edge_weight, node_type_119, node_vec, theta_w, theta_b, phi_w, phi_b,
        W1, b1, W2, b2, emb, adaptW, gamma, beta, W_2, b_2, W_3, b_3, out, stop=None):
    c = Shared()
    c.d, c.r = d, r = Shared(), Shared()
    d.x, d.src, d.dst, d.attr, d.edge_type, d.edge_weight, d.node_type, d.node_vec = (
        x, src, dst, edge_attr_40, edge_type_4, edge_weight, node_type_119, node_vec)
    d.theta_w, d.theta_b, d.phi_w, d.phi_b, d.emb, d.adaptW = theta_w, theta_b, phi_w, phi_b, emb, adaptW
    d.W1, d.b1, d.W2, d.b2, d.gamma, d.beta, d.W_2, d.b_2, d.W_3, d.b_3, d.out = W1, b1, W2, b2, gamma, beta, W_2, b_2, W_3, b_3, out

    def dram(name, shape):
        return nc.dram_tensor(name, shape, F32, kind="Internal").ap()
    d.rows0 = dram("rows0_dram", (NP, W0))
    d.emb_edge = dram("emb_edge_dram", (E, EM))
    d.state = dram("state0_dram", (E + P, H))
    d.state2 = dram("state2_dram", (E + P, H))
    d.spread = dram("spread_dram", (XR * P, WX))
    d.records = dram("records_dram", (XR * P, WR))
    d.rows1 = dram("rows1_dram", (NP, WX))
    d.rows2 = dram("rows2_dram", (NP, H))
    d.rows3 = dram("rows3_dram", (NP * NR, H))

    with ExitStack() as ctx:
        ctx.enter_context(nc.allow_non_contiguous_dma("small loads, one value at a time"))

        def sem(name):
            return ctx.enter_context(nc.semaphore(name))

        def res(name, shape, t=F32):
            return ctx.enter_context(nc.sbuf_tensor("r_" + name, shape, t))
        r.src, r.same, r.dst = res("src", [P, JP], I32), res("same", [P, J]), res("dst", [P, J + 1], I32)
        r.w3, r.lo3, r.row3 = res("w", [P, TP]), res("gidx", [P, TP]), res("pos", [P, TP], I32)
        r.w, r.gidx, r.pos_i = r.w3[:, 0:J], r.lo3[:, 0:J], r.row3[:, 0:J]
        r.gidx_i, r.pos = r.pos_i, r.pos_i.bitcast(F32)
        r.x, r.a, r.e2, r.mult = res("x", [P, NB, H]), res("a", [P, NB, H]), res("e2", [P, NB, EM]), res("mult", [P, NB])
        r.ident, r.ones, r.before, r.iota, r.iota16 = (res("ident", [P, P]), res("ones", [P, P]), res("before", [P, P]), res("iota", [P, P]),
                                                       res("iota16", [P, P], BF16))
        r.part, r.full, r.first_tile, r.deg = res("part", [P, 1]), res("full", [H, P]), res("first_tile", [P, P]), res("deg", [P, NB])
        r.mend_read, r.mend_write, r.first_dst = res("mend_read", [P, 1], I32), res("mend_write", [P, 1], I32), res("first_dst", [P, 1], I32)
        r.dinv = res("dinv", [P, NB])
        r.ends, r.starts = res("ends", [P, NB], I32), res("starts", [P, NB], I32)
        r.cut = r.dst[:, 0:J].bitcast(F32)
        setup(nc, c, sem)
        layer0_tables(nc, c, sem)
        gather_reduce(nc, c, sem, "g0", d.rows0, W0, d.state, True)
        rows_of_dst(nc, c, sem)
        layer0_finish(nc, c, sem)
        if stop == 0:
            return store_x(nc, c, sem)
        layer1_edges(nc, c, sem)
        r.offset = res("offset", [1, T // 13 * 16], I32)
        tile_blocks(nc, c, sem)
        with nc.sbuf_tensor("acc1", [P, NB, H + 1], F32) as acc:
            sum_by_src(nc, c, sem, "s1", None, acc, H + 1)
            layer1_finish(nc, c, sem, acc)
        if stop == 1:
            return store_x(nc, c, sem)
        gather_reduce(nc, c, sem, "g2", d.rows2, H, d.state2, False)
        layer2_finish(nc, c, sem)
        if stop == 2:
            return store_x(nc, c, sem)
        with nc.sbuf_tensor("acc3", [P, NB, H + 1], F32) as acc:
            sum_by_src(nc, c, sem, "s3", d.rows3, acc, H)
            layer3_finish(nc, c, sem, acc)
        store_x(nc, c, sem)


_INS = ['x', 'src', 'dst', 'edge_attr_40', 'edge_type_4', 'edge_weight', 'node_type_119', 'node_vec', 'L0_gnn_theta_w',
        'L0_gnn_theta_b', 'L0_gnn_phi_w', 'L0_gnn_phi_b', 'L1_gnn_W1', 'L1_gnn_b1', 'L1_gnn_W2', 'L1_gnn_b2', 'L1_gnn_emb',
        'L1_gnn_adaptW', 'L1_gnn_gamma', 'L1_gnn_beta', 'L2_gnn_W', 'L2_gnn_b', 'L3_gnn_W', 'L3_gnn_b']
_OUTS = [((12500, 48), 'float32')]


def kernel(**inputs):
    import numpy as _np
    import concourse.bacc as _bacc
    from concourse import mybir as _mybir
    from concourse.bass_utils import run_bass_kernel_spmd as _run

    nc = _bacc.Bacc("TRN2", target_bir_lowering=False, num_devices=1)
    arrays, args = {}, []
    for name in _INS:
        a = _np.ascontiguousarray(inputs[name])
        arrays[f"in_{name}_dram"] = a
        args.append(nc.dram_tensor(f"in_{name}_dram", a.shape, _mybir.dt.from_np(a.dtype), kind="ExternalInput").ap())
    for i, (shape, dtype) in enumerate(_OUTS):
        dt = _mybir.dt.from_np(_np.dtype(dtype))
        args.append(nc.dram_tensor(f"out_{i}_dram", shape, dt, kind="ExternalOutput").ap())
    gnn(nc, *args)
    r = _run(nc, [arrays], core_ids=[0])
    got = tuple(r.results[0][f"out_{i}_dram"] for i in range(len(_OUTS)))
    return got[0]
```

```python
from contextlib import ExitStack

import concourse.bass as bass
from concourse import mybir

ALU = mybir.AluOpType
ACT = mybir.ActivationFunctionType
F32 = mybir.dt.float32
BF16 = mybir.dt.bfloat16
I32 = mybir.dt.int32
AX = mybir.AxisListType.X

P = 128
H = 48
A = 40
EM = 32
NZ = 119
NR = 4
N = 12500
E = 400000
NB = -(-N // P)
NP = NB * P
LAST = N - (NB - 1) * P
J = E // P
B = 24
NI = J // (2 * B)
TAIL = J - 2 * NI * B
T = 3328
BT = 26
SR = 3250
XR = 3380
TP = T + 2 * BT
W0 = H + EM
WX = H + 1 + EM
WM = -(-3 * (H + 1) // 2)
WR = WM + 3
FMAX = 3.4028234663852886e38
EPS = 1e-5
PI = 3.141592653589793
JP = J + 2 * B
assert J * P == E and 2 * NI * B + TAIL == J and T >= J + 2 * NB
assert SR % (2 * NI) == XR % (2 * NI) == 0 and XR >= T and SR * P >= E + NP


class Steps:

    def __init__(self, eng, sem):
        self.eng, self.sem, self.n, self.base = eng, sem, 0, 0

    def __call__(self, ins):
        ins.then_inc(self.sem, 1)
        self.n += 1
        self.eng.wait_ge(self.sem, self.base + self.n)

    def wait_last(self, behind=0):
        self.n += 1
        self.eng.wait_ge(self.sem, self.base + (self.n - behind))

    def enter(self, i, per_turn):
        self.before, self.per_turn = self.n, per_turn
        self.base, self.n = i * per_turn + self.before, 0

    def leave(self, turns):
        assert self.n == self.per_turn, self.n
        self.base, self.n = 0, self.before + turns * self.per_turn


def bc(ap, dim, n):
    shape = list(ap.shape)
    shape[dim] = n
    return ap.to_broadcast(shape)


def nodes(dram):
    return dram.rearrange("(b p) c -> p b c", p=P)


class Shared:
    pass


def load_resident(nc, c, sem):
    d, r = c.d, c.r
    s_w, s_res, s_edge, s_edge_free, s_fill, s_iota, s_const, s_v, s_pe = (
        sem(n) for n in ("weight_loaded", "resident_loaded", "edge_loaded", "edge_cleared", "fill", "iota", "const", "load_dve", "load_pe"))
    with (
        nc.sbuf_tensor("iota_i", [P, P], I32) as iota_i,
        nc.sbuf_tensor("iota_p", [P, 1], I32) as iota_p,
        nc.sbuf_tensor("fall_scratch", [P, J], BF16) as scratch,
        nc.sbuf_tensor("falls", [P, 1], F32) as falls,
        nc.psum_tensor("falls_ps", [P, 512], F32) as falls_ps,
        nc.Block() as block,
    ):
        @block.sync
        def _(sp):
            sp.dma_start(r.src[:, 0:J], d.src.rearrange("(p j) -> p j", p=P)).then_inc(s_edge, 16)
            sp.dma_start(r.dst[:, 1:], d.dst.rearrange("(p j) -> p j", p=P)).then_inc(s_edge, 16)
            sp.wait_ge(s_edge_free, 1)
            sp.dma_start(r.dst[1:P, 0:1], d.dst.rearrange("(p j) -> p j", p=P)[0:P - 1, J - 1:J]).then_inc(s_edge, 16)
            sp.dma_start(r.w, d.edge_weight.rearrange("(p j) -> p j", p=P)).then_inc(s_w, 16)
            sp.dma_start(r.gidx_i, d.edge_type.rearrange("(p j) -> p j", p=P)).then_inc(s_edge, 16)
            sp.wait_ge(s_const, 4)
            for state in (d.state, d.state2):
                sp.dma_start(state[E:E + P, :], r.ones[:, 0:H]).then_inc(s_w, 16)
            sp.wait_ge(s_w, 48)
            sp.wait_ge(s_edge, 64)

        @block.scalar
        def _(act):
            act.wait_ge(s_fill, 2)
            act.dma_start(r.x[:, 0:NB - 1, :], nodes(d.x[0:(NB - 1) * P, :])).then_inc(s_res, 16)
            act.dma_start(r.x[0:LAST, NB - 1, :], d.x[(NB - 1) * P:N, :]).then_inc(s_res, 16)
            act.dma_start(r.mult[:, 0:NB - 1], d.node_vec[0:(NB - 1) * P].rearrange("(b p) -> p b", p=P)).then_inc(s_res, 16)
            act.dma_start(r.mult[0:LAST, NB - 1:NB], d.node_vec[(NB - 1) * P:N].rearrange("(p o) -> p o", o=1)).then_inc(s_res, 16)
            act.wait_ge(s_res, 64)

        @block.gpsimd
        def _(gp):
            gp.iota(iota_i[:, :], pattern=[[1, P]], base=0, channel_multiplier=0).then_inc(s_iota, 1)
            gp.iota(iota_p[:, :], pattern=[[1, 1]], base=0, channel_multiplier=1).then_inc(s_iota, 1)
            gp.memset(r.ident[:, :], 0.0).then_inc(s_const, 1)
            gp.memset(r.ones[:, :], 1.0).then_inc(s_const, 1)
            gp.wait_ge(s_const, 2)
            gp.affine_select(out=r.ident[:, :], in_=r.ident[:, :], compare_op=ALU.not_equal, fill=1.0, base=0,
                             pattern=[[-1, P]], channel_multiplier=1).then_inc(s_const, 1)
            gp.affine_select(out=r.before[:, :], in_=r.ones[:, :], compare_op=ALU.is_gt, fill=0.0, base=0,
                             pattern=[[1, P]], channel_multiplier=-1).then_inc(s_const, 1)

        @block.tensor
        def _(pe):
            pe.wait_ge(s_v, 5)
            pe.matmul(falls_ps[:, 0:1], lhsT=r.ones[:, :], rhs=falls[:, :], start=True, stop=True).then_inc(s_pe, 1)

        @block.vector
        def _(v):
            step = Steps(v, s_v)
            v.memset(r.dst[:, 0:1], -1).then_inc(s_edge_free, 1)
            v.memset(r.x[:, NB - 1, :], 0.0).then_inc(s_fill, 1)
            v.memset(r.mult[:, NB - 1:NB], 0.0).then_inc(s_fill, 1)
            step(v.memset(r.src[:, J:], 0))
            v.wait_ge(s_iota, 2)
            step(v.tensor_copy(r.iota[:, :], iota_i[:, :]))
            step(v.tensor_copy(r.iota16[:, :], iota_i[:, :]))
            step(v.tensor_copy(r.part[:, :], iota_p[:, :]))
            v.wait_ge(s_edge, 64)
            v.wait_ge(s_const, 4)
            step(v.scalar_tensor_tensor(scratch[:, :], r.dst[:, 1:], 1.0, r.dst[:, 0:J], ALU.mult, ALU.is_lt, accum_out=falls[:, :]))
            v.wait_ge(s_pe, 1)
            step(v.tensor_scalar(r.unsorted[:, :], falls_ps[:, 0:1], 1.0, None, ALU.min))


def first_segments(nc, c, sem):
    r = c.r
    s_v, s_pe = sem("first_dve"), sem("first_pe")
    with (
        nc.sbuf_tensor("len_scratch", [P, J], BF16) as scratch,
        nc.sbuf_tensor("small", [P, 8], F32) as small,
        nc.sbuf_tensor("diag", [P, P], F32) as diag,
        nc.psum_tensor("full_ps", [P, 512], F32) as full_ps,
        nc.Block() as block,
    ):
        @block.vector
        def _(v):
            step = Steps(v, s_v)
            step(v.tensor_tensor(r.same[:, :], r.dst[:, 1:], r.dst[:, 0:J], ALU.is_equal))
            step(v.tensor_copy(small[:, 0:1], r.dst[:, 1:2]))
            step(v.tensor_scalar(scratch[:, :], r.dst[:, 1:], small[:, 0:1], 0.0, ALU.is_equal, ALU.add,
                                 accum_out=small[:, 1:2]))
            step(v.tensor_scalar(small[:, 2:3], small[:, 1:2], float(J), r.same[:, 0:1], ALU.is_equal, ALU.mult))
            step(v.tensor_scalar(diag[:, :], r.ident[:, :], small[:, 2:3], None, ALU.mult))
            step(v.tensor_scalar(small[:, 3:4], r.part[:, :], float(J - 1), small[:, 1:2], ALU.mult, ALU.add))
            step(v.tensor_scalar(small[:, 3:4], small[:, 3:4], -1.0, r.same[:, 0:1], ALU.add, ALU.mult))
            step(v.tensor_scalar(small[:, 4:5], r.same[:, 0:1], -float(E), float(E), ALU.mult, ALU.add))
            step(v.tensor_tensor(small[:, 3:4], small[:, 3:4], r.part[:, :], ALU.add))
            step(v.tensor_copy(r.mend_read[:, :], small[:, 3:4]))
            step(v.tensor_tensor(small[:, 4:5], small[:, 4:5], small[:, 3:4], ALU.add))
            step(v.tensor_copy(r.mend_write[:, :], small[:, 4:5]))
            step(v.tensor_copy(r.first_dst[:, :], r.dst[:, 1:2]))
            step(v.scalar_tensor_tensor(r.gidx, r.dst[:, 1:], float(NR), r.gidx_i, ALU.mult, ALU.add))
            v.wait_ge(s_pe, 1)
            step(v.tensor_copy(r.full[:, :], full_ps[0:H, 0:P]))

        @block.tensor
        def _(pe):
            pe.wait_ge(s_v, 5)
            pe.matmul(full_ps[0:H, 0:P], lhsT=r.ones[:, 0:H], rhs=diag[:, :], start=True, stop=True).then_inc(s_pe, 1)


def layernorm_relu(nc, v, step, act_sem, dve_ready, h, x, tmp, stat, relu=True):
    step(v.tensor_reduce(stat[:, 0, :], x, AX, ALU.add))
    step(v.tensor_scalar(stat[:, 0, :], stat[:, 0, :], 1.0 / H, None, ALU.mult))
    step(v.tensor_tensor(h, x, bc(stat[:, 0, :].unsqueeze(2), 2, H), ALU.subtract))
    step(v.tensor_tensor(tmp, h, h, ALU.mult))
    step(v.tensor_reduce(stat[:, 1, :], tmp, AX, ALU.add))
    v.tensor_scalar(stat[:, 1, :], stat[:, 1, :], 1.0 / H, EPS, ALU.mult, ALU.add).then_inc(dve_ready, 1)
    v.wait_ge(*act_sem)
    step(v.reciprocal(stat[:, 3, :], stat[:, 2, :]))
    rstd = bc(stat[:, 3, :].unsqueeze(2), 2, H)
    if relu:
        step(v.scalar_tensor_tensor(h, h, 0.0, rstd, ALU.max, ALU.mult))
    else:
        step(v.tensor_tensor(h, h, rstd, ALU.mult))


def root(nc, act, dve_ready, count, act_sem, stat):
    act.wait_ge(dve_ready, count)
    act.activation(stat[:, 2, :], stat[:, 1, :], ACT.Sqrt).then_inc(act_sem, 1)


class NodeProduct:
    CB = 4
    TURNS = (NB // CB) // 2

    def __init__(self, nc, ctx, sem, name, rhs, width):
        self.rhs, self.width = rhs, width
        self.place = ctx.enter_context(nc.sbuf_tensor(name + "_h", [P, 2, self.CB, H], F32))
        self.hT = ctx.enter_context(nc.sbuf_tensor(name + "_hT", [H, 2, self.CB * P], F32))
        self.tp = [ctx.enter_context(nc.psum_tensor(f"{name}_tp{s}", [H, self.CB * P], F32)) for s in range(2)]
        self.banks = 1 if width <= P else 2
        self.per = self.CB // self.banks
        self.out = [[ctx.enter_context(nc.psum_tensor(f"{name}_o{s}{k}", [P, self.per, 512 // self.per], F32))
                     for k in range(self.banks)] for s in range(2)]
        self.placed, self.turned, self.back, self.made, self.taken, self.pe_go = (
            sem(f"{name}_{n}") for n in ("placed", "turned", "back", "made", "taken", "pe_go"))

    def chunks(self, eng, body):
        with eng.Fori(0, self.TURNS) as i:
            for s in range(2):
                body(i * 2 + s, s, self.CB)
        body(2 * self.TURNS, 0, NB - 2 * self.CB * self.TURNS)

    def on_tensor(self, pe, ident):
        def turn(g, s, nb):
            pe.wait_ge(self.placed, g + 1)
            pe.sem_inc(self.pe_go, 1)
            for b in range(nb):
                last = pe.transpose(self.tp[s][:, b * P:(b + 1) * P], self.place[:, s, b, :], ident[:, :])
            last.then_inc(self.turned, 1)

        def multiply(g, s, nb):
            pe.wait_ge(self.back, g + 3)
            pe.wait_ge(self.taken, g + 1)
            for b in range(nb):
                k, o = divmod(b, self.per)
                last = pe.matmul(self.out[s][k][:, o, 0:self.width], lhsT=self.hT[:, s, b * P:(b + 1) * P], rhs=self.rhs,
                                 start=True, stop=True)
            last.then_inc(self.made, 1)
        turn(0, 0, self.CB)
        with pe.Fori(0, self.TURNS) as i:
            for s in range(2):
                turn(i * 2 + (s + 1), 1 - s, self.CB)
                multiply(i * 2 + s, s, self.CB)
        multiply(2 * self.TURNS, 0, NB - 2 * self.CB * self.TURNS)

    def on_scalar(self, act):
        act.sem_inc(self.back, 2)

        def chunk(g, s, nb):
            act.wait_ge(self.made, g + 1)
            act.wait_ge(self.turned, g + 1)
            act.activation(self.hT[:, s, 0:nb * P], self.tp[s][:, 0:nb * P], ACT.Copy).then_inc(self.back, 1)
        self.chunks(act, chunk)

    def on_vector(self, v, h, take):
        v.sem_inc(self.made, 2)
        v.sem_inc(self.taken, 2)

        def put(g, s, nb):
            v.tensor_scalar(self.place[:, s, 0:nb, :], h[:, bass.ds(g * self.CB, nb), :], 1.0, None, ALU.mult).then_inc(self.placed, 1)

        def get(g, s, nb):
            v.wait_ge(self.made, g + 3)
            rows = [self.out[s][k][:, 0:min(self.per, nb - k * self.per), 0:self.width] for k in range(-(-nb // self.per))]
            take(g, s, nb, rows).then_inc(self.taken, 1)
            v.wait_ge(self.taken, g + 3)
        last = 2 * self.TURNS
        rest = NB - last * self.CB
        put(0, 0, self.CB)
        put(1, 1, self.CB)
        with v.Fori(0, self.TURNS - 1) as i:
            for s in range(2):
                v.wait_ge(self.turned, i * 2 + (s + 1))
                put((i + 1) * 2 + s, s, self.CB)
                get(i * 2 + s, s, self.CB)
        v.wait_ge(self.turned, last - 1)
        put(last, 0, rest)
        get(last - 2, 0, self.CB)
        get(last - 1, 1, self.CB)
        get(last, 0, rest)


def layer0_tables(nc, c, sem):
    d, r = c.d, c.r
    NCH, CB = 7, 14
    CW = CB * P
    with ExitStack() as ctx:
        sb = lambda n, s, t=F32: ctx.enter_context(nc.sbuf_tensor(n, s, t))
        stat = sb("ln_stat", [P, 4, NB])
        wT = sb("w0T", [H, 2 * H])
        phiT = sb("phiT", [H, H])
        bias = sb("bias0", [P, 2, H])
        emb, embT, adT, embs = sb("emb", [NZ, EM]), sb("embT", [EM, NZ]), sb("adaptT", [EM, EM]), sb("embs", [NZ, 2 * EM])
        zrow, zhot = sb("zrow", [NZ, 2, CW], I32), sb("zhot", [NZ, 2, CW])
        rows = sb("rows0", [P, NB, W0])
        zps = [ctx.enter_context(nc.psum_tensor(f"zps{k}", [P, 7, 2 * EM], F32)) for k in range(2)]
        ld, zld, v_s, ready, rt, hs, ps, zh, zm, zt, wr = (
            sem(n) for n in ("l0_weights", "l0_types", "l0_dve", "l0_var", "l0_root", "l0_h", "l0_small_pe", "l0_hot", "l0_hot_mm",
                             "l0_hot_taken", "l0_rows_written"))
        np0 = NodeProduct(nc, ctx, sem, "n0", wT[:, :], 2 * H)
        block = ctx.enter_context(nc.Block())

        @block.sync
        def _(sp):
            sp.dma_start(wT[:, H:], d.theta_w.rearrange("o i -> i o")).then_inc(ld, 16)
            sp.dma_start(phiT[:, :], d.phi_w.rearrange("o i -> i o")).then_inc(ld, 16)
            sp.dma_start(embT[:, :], d.emb.rearrange("z k -> k z")).then_inc(ld, 16)
            sp.dma_start(adT[:, :], d.adaptW.rearrange("o i -> i o")).then_inc(ld, 16)
            sp.dma_start(emb[:, :], d.emb).then_inc(ld, 16)
            sp.dma_start(bias[:, 0, :], bcast_row(d.theta_b)).then_inc(ld, 16)
            sp.dma_start(bias[:, 1, :], bcast_row(d.phi_b)).then_inc(ld, 16)
            for k in range(NCH):
                n = min(CW, N - k * CW)
                if k >= 2:
                    sp.wait_ge(zh, k - 1)
                if n < CW:
                    sp.wait_ge(zt, 1)
                sp.dma_start(zrow[:, k % 2, 0:n], bcast_row(d.node_type[k * CW:k * CW + n], NZ)).then_inc(zld, 16)
                sp.wait_ge(zld, 16 * (k + 1))
            sp.wait_ge(wr, 1)
            sp.dma_start(nodes(d.rows0), rows[:, :, :]).then_inc(ld, 16)
            sp.wait_ge(ld, 16 * 8)

        @block.vector
        def _(v):
            step = Steps(v, v_s)
            layernorm_relu(nc, v, step, (rt, 1), ready, r.a[:, :, :], r.x[:, :, :], rows[:, :, 0:H], stat)
            v.wait_ge(ld, 112)
            step(v.tensor_tensor(wT[:, 0:H], phiT[:, :], wT[:, H:], ALU.subtract))
            step(v.tensor_tensor(bias[:, 0, :], bias[:, 0, :], bias[:, 1, :], ALU.add))
            v.wait_ge(ps, 1)
            step(v.tensor_copy(embs[:, EM:], zps[0][0:NZ, 0, 0:EM]))
            step(v.tensor_copy(embs[:, 0:EM], emb[:, :]))
            v.sem_inc(hs, 1)
            for k in range(NCH):
                if k == NCH - 1:
                    v.memset(zrow[:, k % 2, :], 0).then_inc(zt, 1)
                v.wait_ge(zld, 16 * (k + 1))
                if k >= 2:
                    v.wait_ge(zm, 2 * (k - 1))
                v.tensor_scalar(zhot[:, k % 2, :], zrow[:, k % 2, :], r.part[0:NZ, :], None, ALU.is_equal).then_inc(zh, 1)
                for q in range(2):
                    v.wait_ge(zm, 2 * k + q + 1)
                    b = k * CB + q * 7
                    step(v.tensor_copy(rows[:, b:b + 7, H:], zps[q][:, :, 0:EM]))
                    step(v.tensor_copy(r.e2[:, b:b + 7, :], zps[q][:, :, EM:]))

            def take(g, s, nb, ps_rows):
                v.tensor_scalar(rows[:, bass.ds(g * 4, nb), 0:H], ps_rows[0][:, :, 0:H], 1.0, None, ALU.mult).then_inc(v_s, 1)
                return v.tensor_tensor(r.a[:, bass.ds(g * 4, nb), :], ps_rows[0][:, :, H:], bc(bias[:, 0:1, :], 1, nb), ALU.add)
            np0.on_vector(v, r.a, take)
            v.wait_ge(v_s, step.n + 2 * np0.TURNS + 1)
            v.sem_inc(wr, 1)

        @block.scalar
        def _(act):
            root(nc, act, ready, 1, rt, stat)
            np0.on_scalar(act)

        @block.tensor
        def _(pe):
            pe.wait_ge(ld, 112)
            pe.matmul(zps[0][0:NZ, 0, 0:EM], lhsT=embT[:, :], rhs=adT[:, :], start=True, stop=True).then_inc(ps, 1)
            pe.wait_ge(hs, 1)
            for k in range(NCH):
                pe.wait_ge(zh, k + 1)
                for q in range(2):
                    if k >= 1:
                        pe.wait_ge(v_s, 11 + 4 * (k - 1) + 2 * (q + 1))
                    for b in range(7):
                        o = (q * 7 + b) * P
                        last = pe.matmul(zps[q][:, b, :], lhsT=zhot[:, k % 2, o:o + P], rhs=embs[:, :], start=True, stop=True)
                    last.then_inc(zm, 1)
            np0.on_tensor(pe, r.ident)


def bcast_row(ap, n=P):
    row = ap.rearrange("(o f) -> o f", o=1)
    return row.to_broadcast([n, row.shape[1]])


def sort_by_dst(nc, c, sem):
    d, r = c.d, c.r
    GB = 25
    GN = J // GB
    assert GB * GN == J
    F = 8
    with ExitStack() as ctx:
        sb = lambda n, s, t=F32: ctx.enter_context(nc.sbuf_tensor("so_" + n, s, t))
        orig, key, mask, scan, pos = sb("orig", [P, J]), sb("key", [P, J], BF16), sb("mask", [P, J], BF16), sb("scan", [P, J]), sb("pos", [P, J])
        cnt, tot, start, here = (sb(n, [P, P]) for n in ("cnt", "tot", "start", "here"))
        rec, idx, before_first = sb("rec", [P, GB, F]), sb("idx", [P, GB], I32), sb("before_first", [P, 1])
        rows = sb("rows", [P, GB, A])
        scan_i = scan[:, :].bitcast(I32)
        ps = ctx.enter_context(nc.psum_tensor("so_ps", [P, 2, 256], F32))

        it, od = sem("so_iota"), sem("so_orig")
        with nc.Block() as block:
            @block.gpsimd
            def _(gp):
                gp.iota(scan_i, pattern=[[1, J]], base=0, channel_multiplier=J).then_inc(it, 1)

            @block.vector
            def _(v):
                v.wait_ge(it, 1)
                v.tensor_copy(orig[:, :], scan_i).then_inc(od, 1)
                v.wait_ge(od, 1)

            @block.scalar
            def _(act):
                act.wait_ge(od, 1)

            @block.tensor
            def _(pe):
                pe.wait_ge(od, 1)

            @block.sync
            def _(sp):
                sp.wait_ge(od, 1)

        for digit in range(2):
            name = f"so{digit}_"
            dv, counted, based = sem(name + "dve"), sem(name + "counted"), sem(name + "based")
            with nc.Block() as block:
                @block.tensor
                def _(pe):
                    pe.wait_ge(counted, 1)
                    pe.matmul(ps[:, 0, 0:P], lhsT=r.ones[:, :], rhs=cnt[:, :], start=True, stop=True)
                    pe.matmul(ps[:, 1, 0:P], lhsT=r.before[:, :], rhs=cnt[:, :], start=True, stop=True).then_inc(based, 1)

                @block.vector
                def _(v):
                    step = Steps(v, dv)
                    if digit == 0:
                        step(v.tensor_scalar(scan_i, r.dst[:, 1:], P - 1, None, ALU.bitwise_and))
                    else:
                        step(v.tensor_scalar(scan_i, r.dst[:, 1:], 7, None, ALU.arith_shift_right))
                    step(v.tensor_copy(key[:, :], scan_i))
                    step(v.memset(cnt[:, :], 0.0))
                    step(v.memset(pos[:, :], 0.0))
                    with v.Fori(0, P) as b:
                        step.enter(b, 1)
                        step(v.tensor_scalar(mask[:, :], key[:, :], r.iota[:, bass.ds(b, 1)], 0.0, ALU.is_equal, ALU.add,
                                             accum_out=cnt[:, bass.ds(b, 1)]))
                    step.leave(P)
                    v.sem_inc(counted, 1)
                    v.wait_ge(based, 1)
                    step(v.tensor_copy(tot[:, :], ps[:, 0, 0:P]))
                    step(v.tensor_tensor_scan(start[:, :], tot[:, :], tot[:, :], 0.0, ALU.add, ALU.bypass))
                    step(v.tensor_tensor(start[:, :], start[:, :], tot[:, :], ALU.subtract))
                    step(v.scalar_tensor_tensor(here[:, :], start[:, :], -1.0, ps[:, 1, 0:P], ALU.add, ALU.add))
                    with v.Fori(0, P) as b:
                        step.enter(b, 4)
                        step(v.tensor_scalar(mask[:, :], key[:, :], r.iota[:, bass.ds(b, 1)], None, ALU.is_equal))
                        step(v.tensor_tensor_scan(scan[:, :], mask[:, :], mask[:, :], here[:, bass.ds(b, 1)], ALU.add, ALU.bypass))
                        step(v.scalar_tensor_tensor(scan[:, :], key[:, :], r.iota[:, bass.ds(b, 1)], scan[:, :], ALU.is_equal, ALU.mult))
                        step(v.tensor_tensor(pos[:, :], pos[:, :], scan[:, :], ALU.add))
                    step.leave(P)
                    step(v.tensor_copy(scan_i, pos[:, :]))

            array = d.sorted_records[digit]
            dv2, ready, moved, go = sem(name + "dve2"), sem(name + "ready"), sem(name + "moved"), sem(name + "go")
            with nc.Block() as block:
                @block.vector
                def _(v):
                    step = Steps(v, dv2)
                    step(v.memset(rec[:, :, :], 0.0))
                    with v.Fori(0, GN) as i:
                        step.enter(i, 6)
                        cols, shifted = bass.ds(i * GB, GB), bass.ds(i * GB + 1, GB)
                        for k, part in enumerate((r.src[:, cols], r.dst[:, shifted], r.gidx_i[:, cols], r.w[:, cols], orig[:, cols])):
                            step(v.tensor_scalar(rec[:, :, k], part, 1.0, None, ALU.mult))
                        step(v.tensor_scalar(idx[:, :], scan_i[:, cols], 0.0, None, ALU.add))
                        v.sem_inc(ready, 1)
                        v.wait_ge(moved, i * (16 * GB) + 16 * GB)
                    step.leave(GN)

                @block.gpsimd
                def _(gp):
                    with gp.Fori(0, GN) as i:
                        gp.wait_ge(ready, i + 1)
                        gp.sem_inc(go, 1)
                        for b in range(GB):
                            gp.indirect_dma_start(array, bass.IndirectOffsetOnAxis(ap=idx[:, b:b + 1], axis=0), rec[:, b, :], None).then_inc(moved, 16)

            ld, conv = sem(name + "field_in"), sem(name + "field_taken")
            cleared = sem(name + "cleared")
            with nc.Block() as block:
                @block.sync
                def _(sp):
                    fields = array.rearrange("(p j) c -> p j c", p=P)
                    for k in range(5):
                        if k:
                            sp.wait_ge(conv, k)
                        sp.dma_start(pos[:, :], fields[:, :, k]).then_inc(ld, 16)
                        sp.wait_ge(ld, 16 * (k + 1))
                    sp.wait_ge(cleared, 1)
                    sp.dma_start(before_first[1:P, :], fields[0:P - 1, J - 1, 1:2]).then_inc(ld, 16)
                    sp.wait_ge(ld, 96)

                @block.vector
                def _(v):
                    v.memset(before_first[:, :], -1.0).then_inc(cleared, 1)
                    for k, to in enumerate((r.src[:, 0:J], r.dst[:, 1:], r.gidx_i, r.w, orig[:, :])):
                        v.wait_ge(ld, 16 * (k + 1))
                        v.tensor_copy(to, pos[:, :]).then_inc(conv, 1)
                    v.wait_ge(ld, 96)
                    v.tensor_copy(r.dst[:, 0:1], before_first[:, :]).then_inc(conv, 1)
                    v.wait_ge(conv, 6)

        ready, gathered, stored, go = (sem("so_" + n) for n in ("attr_ready", "attr_gathered", "attr_stored", "attr_go"))
        with nc.Block() as block:
            @block.vector
            def _(v):
                with v.Fori(0, GN) as i:
                    v.tensor_scalar(idx[:, :], orig[:, bass.ds(i * GB, GB)], 0.0, None, ALU.add).then_inc(ready, 1)
                    v.wait_ge(stored, i * 16 + 16)

            @block.gpsimd
            def _(gp):
                with gp.Fori(0, GN) as i:
                    gp.wait_ge(ready, i + 1)
                    gp.sem_inc(go, 1)
                    for b in range(GB):
                        gp.indirect_dma_start(rows[:, b, :], None, d.attr, bass.IndirectOffsetOnAxis(ap=idx[:, b:b + 1], axis=0)).then_inc(gathered, 16)

            @block.sync
            def _(sp):
                attr_v = d.attr_sorted.rearrange("(p j) c -> p j c", p=P)
                with sp.Fori(0, GN) as i:
                    sp.wait_ge(gathered, i * (16 * GB) + 16 * GB)
                    sp.dma_start(attr_v[:, bass.ds(i * GB, GB), :], rows[:, :, :]).then_inc(stored, 16)
                sp.wait_ge(stored, 16 * GN)


def gather_reduce(nc, c, sem, name, table, width, state_dram, largest):
    d, r = c.d, c.r
    first = largest
    HB = B // 2
    QB = 4
    TA = NI - NB // 2
    assert TA * 2 * QB >= NB and TA * 2 * QB <= P and NB % 2 == 0
    with ExitStack() as ctx:
        sb = lambda n, s, t=F32: ctx.enter_context(nc.sbuf_tensor(name + n, s, t))
        ring, idx, state, flag = sb("ring", [P, 2, B, width]), sb("idx", [P, 2, B], I32), sb("state", [P, 2, B, H]), sb("flag", [P, 2, B])
        gathered = [sem(f"{name}_gathered{s}") for s in range(2)]
        stored = [sem(f"{name}_state_stored{s}") for s in range(2)]
        kept = [sem(f"{name}_emb_stored{s}") for s in range(2)]
        idx_ready, pool_go, state_ready, emb_ready, dv = (sem(f"{name}_{n}") for n in ("idx_ready", "pool_go", "state_ready", "emb_ready", "dve"))
        if first:
            emb = sb("emb", [P, 2, B, EM])
            hot = sb("hot", [P, 2, HB, P + NB], BF16)
            dsti = sb("dsti", [P, 2, B], I32)
            key, mask, scan = sb("key", [P, J], BF16), sb("mask", [P, J], BF16), sb("scan", [P, J])
            keyi = scan[:, :].bitcast(I32)
            cnt, tot, tiles_i, start, here = sb("cnt", [P, P]), sb("tot", [P, P]), sb("tiles_i", [P, P], I32), sb("start", [P, P]), sb("here", [P, P])
            zero = sb("zero", [P, max(SR * WX, XR * WR) // (2 * NI)])
            zb = sb("zb", [P, P], BF16)
            cnt_ps = ctx.enter_context(nc.psum_tensor(name + "cnt_ps", [P, 512], F32))
            base_ps = ctx.enter_context(nc.psum_tensor(name + "base_ps", [P, 2, 256], F32))
            hot_ready, hot_used, counted, base_made, zeroed, zero_ready, pe_done = (
                sem(f"{name}_{n}") for n in ("hot_ready", "hot_used", "counted", "base_made", "zeroed", "zero_ready", "pe_done"))
        block = ctx.enter_context(nc.Block())

        @block.gpsimd
        def _(gp):
            def gather(s, nb):
                for b in range(nb):
                    gp.indirect_dma_start(ring[:, s, b, :], None, table,
                                          bass.IndirectOffsetOnAxis(ap=idx[:, s, b:b + 1], axis=0)).then_inc(gathered[s], 16)
            with gp.Fori(0, NI) as i:
                for s in range(2):
                    gp.wait_ge(idx_ready, i * 2 + (s + 1))
                    gp.sem_inc(pool_go, 1)
                    gather(s, B)
            gp.wait_ge(idx_ready, 2 * NI + 1)
            gather(0, TAIL)

        @block.sync
        def _(sp):
            state_v = state_dram[0:E, :].rearrange("(p j) c -> p j c", p=P)
            emb_v = d.emb_edge.rearrange("(p j) c -> p j c", p=P) if first else None
            for s in range(2):
                sp.sem_inc(stored[s], 16)
                if first:
                    sp.sem_inc(kept[s], 16)

            def store(g, s, nb):
                if first:
                    sp.wait_ge(emb_ready, g + 1)
                    sp.dma_start(emb_v[:, bass.ds(g * B, nb), :], emb[:, s, 0:nb, :]).then_inc(kept[s], 16)
                sp.wait_ge(state_ready, g + 1)
                sp.dma_start(state_v[:, bass.ds(g * B, nb), :], state[:, s, 0:nb, :]).then_inc(stored[s], 16)
            with sp.Fori(0, NI) as i:
                for s in range(2):
                    store(i * 2 + s, s, B)
            store(2 * NI, 0, TAIL)
            for s in range(2):
                sp.wait_ge(stored[s], 16 * (NI + 2 - s))
                if first:
                    sp.wait_ge(kept[s], 16 * (NI + 2 - s))

        @block.vector
        def _(v):
            step = Steps(v, dv)
            neutral = -FMAX if largest else 0.0
            op0, op1 = (ALU.min, ALU.max) if largest else (ALU.mult, ALU.add)

            def stage(g, s):
                v.tensor_scalar(idx[:, s, :], r.src[:, bass.ds(g * B, B)], 0.0, None, ALU.add).then_inc(idx_ready, 1)

            def reduce(i, s, nb):
                g = i * 2 + s
                if largest:
                    step(v.tensor_scalar(flag[:, s, 0:nb], r.same[:, bass.ds(g * B, nb)], 2.0, -1.0, ALU.mult, ALU.add))
                    step(v.tensor_scalar(flag[:, s, 0:nb], flag[:, s, 0:nb], FMAX, None, ALU.mult))
                else:
                    step(v.tensor_scalar(flag[:, s, 0:nb], r.same[:, bass.ds(g * B, nb)], 1.0, None, ALU.mult))
                if first:
                    for q, (op, val) in enumerate(((ALU.arith_shift_right, 7), (ALU.bitwise_and, P - 1))):
                        step(v.tensor_scalar(dsti[:, q, 0:nb], r.dst[:, bass.ds(g * B + 1, nb)], val, None, op))
                v.wait_ge(gathered[s], (i + 1) * (16 * B) if nb == B else NI * 16 * B + 16 * nb)
                v.wait_ge(stored[s], i * 16 + 16)
                for b in range(nb):
                    prev = state[:, s, b - 1, :] if b else state[:, 1 - s, B - 1, :]
                    v.scalar_tensor_tensor(state[:, s, b, :], prev, flag[:, s, b:b + 1], ring[:, s, b, 0:H], op0, op1).then_inc(dv, 1)
                    if first:
                        half, k = divmod(b, HB)
                        if k == 0:
                            v.wait_ge(hot_used, i * 4 + (2 * s + half + 1))
                        v.tensor_scalar(hot[:, half, k, 0:P], r.iota16[:, :], dsti[:, 1, b:b + 1], None, ALU.is_equal)
                        hot_last = v.tensor_scalar(hot[:, half, k, P:], r.iota16[:, 0:NB], dsti[:, 0, b:b + 1], None, ALU.is_equal)
                        if k == HB - 1 or b == nb - 1:
                            hot_last.then_inc(hot_ready, 1)
                    step.wait_last()
                v.sem_inc(state_ready, 1)

            step(v.memset(state[:, 1, B - 1, :], neutral))
            if first:
                v.memset(zero[:, :], 0.0).then_inc(zero_ready, 1)
            for s in range(2):
                stage(s, s)
            if first:
                v.sem_inc(hot_used, 2)
                step(v.memset(cnt[:, :], 0.0))
                v.memset(zb[:, :], 0.0).then_inc(zero_ready, 1)
                step(v.tensor_scalar(keyi, r.src[:, 0:J], 7, None, ALU.arith_shift_right))
                step(v.tensor_copy(key[:, :], keyi))

            def turn(i, extra):
                for s in range(2):
                    reduce(i, s, B)
                    if first:
                        v.wait_ge(emb_ready, i * 2 + (s + 1))
                    stage((i + 1) * 2 + s, s)
                    if first:
                        extra(i, s)

            if not first:
                with v.Fori(0, NI) as i:
                    step.enter(i, 2 * (B + 1))
                    turn(i, None)
                step.leave(NI)
                reduce(NI, 0, TAIL)
            else:
                def count_blocks(i, s):
                    for q in range(QB):
                        b = (i * 2 + s) * QB + q
                        step(v.tensor_scalar(mask[:, :], key[:, :], r.iota[:, bass.ds(b, 1)], 0.0, ALU.is_equal, ALU.add,
                                             accum_out=cnt[:, bass.ds(b, 1)]))

                def rank_block(i, s):
                    b = (i - TA) * 2 + s
                    step(v.tensor_scalar(mask[:, :], key[:, :], r.iota[:, bass.ds(b, 1)], None, ALU.is_equal))
                    step(v.tensor_tensor_scan(scan[:, :], mask[:, :], mask[:, :], here[:, bass.ds(b, 1)], ALU.add, ALU.bypass))
                    step(v.scalar_tensor_tensor(scan[:, :], key[:, :], r.iota[:, bass.ds(b, 1)], scan[:, :], ALU.is_equal, ALU.mult))
                    step(v.tensor_tensor(r.pos, r.pos, scan[:, :], ALU.add))

                with v.Fori(0, TA) as i:
                    step.enter(i, 2 * (B + 4 + QB))
                    turn(i, count_blocks)
                step.leave(TA)
                v.sem_inc(counted, 1)
                v.wait_ge(base_made, 1)
                step(v.tensor_scalar(tot[:, :], base_ps[:, 0, 0:P], float(2 * P - 1), None, ALU.add))
                step(v.tensor_copy(tiles_i[:, :], tot[:, :]))
                step(v.tensor_scalar(tiles_i[:, :], tiles_i[:, :], 8, None, ALU.arith_shift_right))
                step(v.tensor_copy(tot[:, :], tiles_i[:, :]))
                step(v.tensor_scalar(tot[:, :], tot[:, :], 1.0, 2.0, ALU.max, ALU.mult))
                step(v.tensor_tensor_scan(start[:, :], tot[:, :], tot[:, :], 0.0, ALU.add, ALU.bypass))
                step(v.tensor_tensor(r.first_tile[:, :], start[:, :], tot[:, :], ALU.subtract))
                step(v.tensor_scalar(start[:, :], r.first_tile[:, :], float(P), -1.0, ALU.mult, ALU.add))
                step(v.tensor_tensor(here[:, :], start[:, :], base_ps[:, 1, 0:P], ALU.add))
                step(v.memset(r.pos, 0.0))
                with v.Fori(TA, NI) as i:
                    step.enter(i - TA, 2 * (B + 4 + 4))
                    turn(i, rank_block)
                step.leave(NI - TA)
                reduce(NI, 0, TAIL)
                v.wait_ge(pe_done, 1)
                step(v.tensor_copy(r.deg[:, :], cnt_ps[:, 0:NB]))
                step(v.tensor_copy(r.pos_i, r.pos))
                step(v.tensor_scalar(keyi, r.pos_i, P - 1, None, ALU.bitwise_and))
                step(v.tensor_scalar(r.pos_i, r.pos_i, 7, None, ALU.arith_shift_right))
                step(v.scalar_tensor_tensor(r.pos_i, keyi, float(XR), r.pos_i, ALU.mult, ALU.add))

        if first:
            @block.scalar
            def _(act):
                def keep(i, s, nb):
                    act.wait_ge(gathered[s], (i + 1) * (16 * B) if nb == B else NI * 16 * B + 16 * nb)
                    act.wait_ge(kept[s], i * 16 + 16)
                    act.activation(emb[:, s, 0:nb, :], ring[:, s, 0:nb, H:], ACT.Copy).then_inc(emb_ready, 1)
                act.wait_ge(zero_ready, 2)
                with act.Fori(0, NI) as i:
                    for s in range(2):
                        keep(i, s, B)
                        for array, rows, width in ((d.spread, SR, WX), (d.records, XR, WR)):
                            part = rows // (2 * NI) * width
                            act.dma_start(array.rearrange("(p j) c -> p (j c)", p=P)[:, bass.ds((i * 2 + s) * part, part)],
                                          zero[:, 0:part]).then_inc(zeroed, 16)
                keep(NI, 0, TAIL)
                act.wait_ge(zeroed, 64 * NI)

            @block.tensor
            def _(pe):
                pe.wait_ge(zero_ready, 2)
                pe.matmul(cnt_ps[:, 0:NB], lhsT=zb[:, :], rhs=zb[:, 0:NB], start=True, stop=False, skip_group_check=True)

                def columns(i, s, half, nb):
                    pe.wait_ge(hot_ready, i * 4 + (2 * s + half + 1))
                    for b in range(nb):
                        last = pe.matmul(cnt_ps[:, 0:NB], lhsT=hot[:, half, b, 0:P], rhs=hot[:, half, b, P:], start=False, stop=False,
                                         skip_group_check=True)
                    last.then_inc(hot_used, 1)

                def turns(lo, hi):
                    with pe.Fori(lo, hi) as i:
                        for s in range(2):
                            for half in range(2):
                                columns(i, s, half, HB)
                turns(0, TA)
                pe.wait_ge(counted, 1)
                pe.matmul(base_ps[:, 0, 0:P], lhsT=r.ones[:, :], rhs=cnt[:, :], start=True, stop=True)
                pe.matmul(base_ps[:, 1, 0:P], lhsT=r.before[:, :], rhs=cnt[:, :], start=True, stop=True).then_inc(base_made, 1)
                turns(TA, NI)
                columns(NI, 0, 0, TAIL)
                pe.matmul(cnt_ps[:, 0:NB], lhsT=zb[:, :], rhs=zb[:, 0:NB], start=False, stop=True, skip_group_check=True).then_inc(pe_done, 1)


def mend_and_take(nc, c, sem, name, state_dram, largest, ends, out):
    r = c.r
    with ExitStack() as ctx:
        sb = lambda n, s, t=F32: ctx.enter_context(nc.sbuf_tensor(name + n, s, t))
        last, lastT, flagT, carry, carried, row = (sb("last", [P, H]), sb("lastT", [H, P]), sb("flagT", [H, P]), sb("carry", [H, P + 1]),
                                                   sb("carried", [P, H]), sb("row", [P, H]))
        tps = ctx.enter_context(nc.psum_tensor(name + "t", [P, 512], F32))
        t2s = ctx.enter_context(nc.psum_tensor(name + "t2", [P, 512], F32))
        ld, rd, dv, pt, mended, taken, started, stored = (sem(f"{name}_{n}") for n in ("last", "row", "dve", "pe", "mended", "taken", "started", "stored"))
        block = ctx.enter_context(nc.Block())

        @block.sync
        def _(sp):
            sp.dma_start(last[:, :], state_dram[0:E, :].rearrange("(p j) c -> p j c", p=P)[:, J - 1, :]).then_inc(ld, 16)
            sp.wait_ge(ld, 16)

        @block.tensor
        def _(pe):
            pe.wait_ge(ld, 16)
            pe.transpose(tps[0:H, 0:P], last[:, :], r.ident[:, :]).then_inc(pt, 1)
            pe.wait_ge(started, 1)
            pe.transpose(t2s[:, 0:H], carry[:, 0:P], r.ident[0:H, 0:H]).then_inc(pt, 1)

        @block.vector
        def _(v):
            step = Steps(v, dv)
            if largest:
                step(v.tensor_scalar(flagT[:, :], r.full[:, :], 2.0, -1.0, ALU.mult, ALU.add))
                step(v.tensor_scalar(flagT[:, :], flagT[:, :], FMAX, None, ALU.mult))
            else:
                step(v.tensor_copy(flagT[:, :], r.full[:, :]))
            neutral = -FMAX if largest else 0.0
            step(v.memset(carry[:, 0:1], neutral))
            v.wait_ge(pt, 1)
            step(v.tensor_copy(lastT[:, :], tps[0:H, 0:P]))
            step(v.tensor_tensor_scan(carry[:, 1:], flagT[:, :], lastT[:, :], neutral, ALU.min if largest else ALU.mult, ALU.max if largest else ALU.add))
            v.sem_inc(started, 1)
            v.wait_ge(pt, 2)
            step(v.tensor_copy(carried[:, :], t2s[:, 0:H]))
            v.wait_ge(rd, 16)
            step(v.tensor_tensor(row[:, :], row[:, :], carried[:, :], ALU.max if largest else ALU.add))
            v.sem_inc(mended, 1)

        @block.gpsimd
        def _(gp):
            gp.indirect_dma_start(row[:, :], None, state_dram, bass.IndirectOffsetOnAxis(ap=r.mend_read[:, :], axis=0)).then_inc(rd, 16)
            gp.wait_ge(mended, 1)
            gp.indirect_dma_start(state_dram, bass.IndirectOffsetOnAxis(ap=r.mend_write[:, :], axis=0), row[:, :], None).then_inc(stored, 16)
            gp.wait_ge(stored, 16)
            for b in range(NB):
                gp.indirect_dma_start(out[:, b, :], None, state_dram, bass.IndirectOffsetOnAxis(ap=ends[:, b:b + 1], axis=0)).then_inc(taken, 16)
            gp.wait_ge(taken, 16 * NB)


def rows_of_dst(nc, c, sem):
    r = c.r
    with (
        nc.sbuf_tensor("rd_a", [P, 5, NB], F32) as w,
        nc.sbuf_tensor("rd_node", [P, NB], I32) as node,
        nc.psum_tensor("rd_ps", [P, 2, 256], F32) as ps,
        nc.Block() as block,
    ):
        pt, dv, it = sem("rd_pe"), sem("rd_dve"), sem("rd_iota")

        @block.gpsimd
        def _(gp):
            gp.iota(node[:, :], pattern=[[P, NB]], base=E, channel_multiplier=1).then_inc(it, 1)

        @block.tensor
        def _(pe):
            pe.matmul(ps[:, 0, 0:NB], lhsT=r.before[:, :], rhs=r.deg[:, :], start=True, stop=True)
            pe.matmul(ps[:, 1, 0:NB], lhsT=r.ones[:, :], rhs=r.deg[:, :], start=True, stop=True).then_inc(pt, 1)

        @block.vector
        def _(v):
            step = Steps(v, dv)
            v.wait_ge(pt, 1)
            step(v.tensor_copy(w[:, 0, :], ps[:, 1, 0:NB]))
            step(v.tensor_tensor_scan(w[:, 1, :], w[:, 0, :], w[:, 0, :], 0.0, ALU.add, ALU.bypass))
            step(v.tensor_tensor(w[:, 1, :], w[:, 1, :], w[:, 0, :], ALU.subtract))
            step(v.tensor_tensor(w[:, 1, :], w[:, 1, :], ps[:, 0, 0:NB], ALU.add))
            step(v.scalar_tensor_tensor(w[:, 2, :], w[:, 1, :], -1.0, r.deg[:, :], ALU.add, ALU.add))
            step(v.tensor_scalar(r.ends[:, :], w[:, 2, :], 0.0, None, ALU.max))
            v.wait_ge(it, 1)
            step(v.tensor_tensor(w[:, 3, :], node[:, :], w[:, 1, :], ALU.subtract))
            step(v.scalar_tensor_tensor(w[:, 3, :], r.deg[:, :], 0.0, w[:, 3, :], ALU.is_equal, ALU.mult))
            step(v.tensor_tensor(r.starts[:, :], w[:, 3, :], w[:, 1, :], ALU.add))


def layer0_finish(nc, c, sem):
    d, r = c.d, c.r
    with ExitStack() as ctx:
        took = ctx.enter_context(nc.sbuf_tensor("took0", [P, NB, H], F32))
        mend_and_take(nc, c, sem, "m0", d.state, True, r.ends, took)
        stat = ctx.enter_context(nc.sbuf_tensor("stat1", [P, 4, NB], F32))
        rows = ctx.enter_context(nc.sbuf_tensor("rows1", [P, NB, WX], F32))
        block = ctx.enter_context(nc.Block())
        dv, ready, rt, rows_ready, wr, angle, sine = (sem("f0_" + n) for n in ("dve", "var", "root", "rows", "written", "angle", "sine"))

        @block.vector
        def _(v):
            step = Steps(v, dv)
            step(v.tensor_tensor(r.a[:, :, :], r.a[:, :, :], took[:, :, :], ALU.add))
            step(v.tensor_scalar(stat[:, 0, :], r.deg[:, :], 0.0, None, ALU.is_gt))
            step(v.tensor_tensor(r.a[:, :, :], r.a[:, :, :], bc(stat[:, 0, :].unsqueeze(2), 2, H), ALU.mult))
            step(v.tensor_tensor(r.x[:, :, :], r.x[:, :, :], r.a[:, :, :], ALU.add))
            step(v.tensor_copy(rows[:, :, H], r.mult[:, :]))
            step(v.tensor_copy(rows[:, :, H + 1:], r.e2[:, :, :]))
            layernorm_relu(nc, v, step, (rt, 1), ready, r.a[:, :, :], r.x[:, :, :], took[:, :, :], stat)
            step(v.tensor_copy(rows[:, :, 0:H], r.a[:, :, :]))
            v.sem_inc(rows_ready, 1)
            cut = r.cut
            step(v.scalar_tensor_tensor(cut, r.w, -1.0, r.w, ALU.mult, ALU.max))
            step(v.tensor_scalar(cut, cut, 6.0, -PI / 6.0, ALU.min, ALU.mult))
            step(v.tensor_scalar(cut, cut, PI / 2.0, None, ALU.add))
            v.sem_inc(angle, 1)
            v.wait_ge(sine, 1)
            step(v.tensor_scalar(cut, cut, 0.5, 0.5, ALU.mult, ALU.add))
            step(v.scalar_tensor_tensor(cut, r.w, 6.0, cut, ALU.is_lt, ALU.mult))

        @block.scalar
        def _(act):
            root(nc, act, ready, 1, rt, stat)
            act.wait_ge(angle, 1)
            act.activation(r.cut, r.cut, ACT.Sin).then_inc(sine, 1)

        @block.sync
        def _(sp):
            sp.wait_ge(rows_ready, 1)
            sp.dma_start(nodes(d.rows1), rows[:, :, :]).then_inc(wr, 16)
            sp.wait_ge(wr, 16)

        @block.gpsimd
        def _(gp):
            gp.wait_ge(rows_ready, 1)
            sc = sem("f0_scattered")
            for b in range(NB):
                gp.indirect_dma_start(d.spread, bass.IndirectOffsetOnAxis(ap=r.starts[:, b:b + 1], axis=0), rows[:, b, :], None).then_inc(sc, 16)
            gp.wait_ge(sc, 16 * NB)


def store_x(nc, c, sem):
    d, r = c.d, c.r
    done = sem("out_stored")
    with nc.Block() as block:
        @block.sync
        def _(sp):
            sp.dma_start(nodes(d.out[0:(NB - 1) * P, :]), r.x[:, 0:NB - 1, :]).then_inc(done, 16)
            sp.dma_start(d.out[(NB - 1) * P:N, :], r.x[0:LAST, NB - 1, :]).then_inc(done, 16)
            sp.wait_ge(done, 32)


def layer1_edges(nc, c, sem):
    d, r = c.d, c.r
    SB = 8
    KB = B // SB
    with ExitStack() as ctx:
        sb = lambda n, s, t=F32: ctx.enter_context(nc.sbuf_tensor("e1" + n, s, t))
        spread, attr, emb = sb("spread", [P, 2, B, WX]), sb("attr", [P, 2, B, A]), sb("emb", [P, 2, B, EM])
        row = sb("row", [P, 2, B, WX])
        same = sb("same", [P, 2, B])
        prod, logit, coef, gate, lo = sb("prod", [P, B, EM]), sb("logit", [P, B]), sb("coef", [P, B]), sb("gate", [P, SB, H]), sb("lo", [P, B], I32)
        rec, slot = sb("rec", [P, 2, B, WR]), sb("slot", [P, 2, B], I32)
        message = sb("message", [P, B, H + 1])
        thirds = rec[:, :, :, 0:WM].bitcast(BF16)
        w1, w2, b1 = sb("w1", [2 * A, 2 * H]), sb("w2", [2 * H + 1, 2 * H]), sb("b1", [2 * H, 1])
        attrT, hidden = sb("attrT", [2 * A, 2, SB // 2 * P]), sb("hidden", [2 * H + 1, 2, SB // 2 * P])
        ps = lambda n: [ctx.enter_context(nc.psum_tensor(f"e1{n}{s}", [P, 512], F32)) for s in range(2)]
        tp, hp, gp_ps = ps("tp"), ps("hp"), ps("gp")
        two = lambda n: [sem(f"e1_{n}{s}") for s in range(2)]
        spread_in, attr_in, emb_in, scattered = two("spread_in"), two("attr_in"), two("emb_in"), two("scattered")
        (w_in, cleared, first_row, spread_used, emb_used, turned, turned_back, hid, act_done, gated, gate_used, rec_ready, pool_go,
         dv, sp_go) = (sem("e1_" + n) for n in ("w_in", "cleared", "first_row", "spread_used", "emb_used", "turned", "turned_back",
                                              "hid", "act_done", "gated", "gate_used", "rec_ready", "pool_go", "dve", "sp_go"))
        block = ctx.enter_context(nc.Block())

        @block.sync
        def _(sp):
            spread_v = d.spread[0:E, :].rearrange("(p j) c -> p j c", p=P)
            attr_v, attr_sorted_v = (a.rearrange("(p j) c -> p j c", p=P) for a in (d.attr, d.attr_sorted))
            unsorted = nc.values_load(r.unsorted[0:1, 0:1], engines=[sp.engine], min_val=0, max_val=1)
            emb_v = d.emb_edge.rearrange("(p j) c -> p j c", p=P)
            sp.wait_ge(cleared, 2)
            for k in range(2):
                sp.dma_start(w1[k * A:(k + 1) * A, k * H:(k + 1) * H], d.W1.rearrange("o i -> i o")).then_inc(w_in, 16)
                sp.dma_start(w2[k * H:(k + 1) * H, k * H:(k + 1) * H], d.W2.rearrange("o i -> i o")).then_inc(w_in, 16)
                sp.dma_start(w2[2 * H:2 * H + 1, k * H:(k + 1) * H], d.b2.rearrange("(o f) -> o f", o=1)).then_inc(w_in, 16)
                sp.dma_start(b1[k * H:(k + 1) * H, :], d.b1.rearrange("(f o) -> f o", o=1)).then_inc(w_in, 16)

            def load(g, s, nb):
                sp.wait_ge(turned, g * KB + 1)
                sp.sem_inc(sp_go, 1)
                with sp.If(unsorted > 0):
                    sp.dma_start(attr[:, s, 0:nb, :], attr_sorted_v[:, bass.ds(g * B, nb), :]).then_inc(attr_in[s], 16)
                with sp.Else():
                    sp.dma_start(attr[:, s, 0:nb, :], attr_v[:, bass.ds(g * B, nb), :]).then_inc(attr_in[s], 16)
                sp.wait_ge(spread_used, g + 1)
                sp.dma_start(spread[:, s, 0:nb, :], spread_v[:, bass.ds(g * B, nb), :]).then_inc(spread_in[s], 16)
                sp.wait_ge(emb_used, g + 1)
                sp.dma_start(emb[:, s, 0:nb, :], emb_v[:, bass.ds(g * B, nb), :]).then_inc(emb_in[s], 16)
            with sp.Fori(0, NI) as i:
                for s in range(2):
                    load(i * 2 + s, s, B)
            load(2 * NI, 0, TAIL)
            for s in range(2):
                for q in (attr_in, spread_in, emb_in):
                    sp.wait_ge(q[s], 16 * (NI + 1 - s))
            sp.wait_ge(w_in, 128)

        @block.tensor
        def _(pe):
            pe.sem_inc(hid, 2)
            pe.sem_inc(gated, 2)
            pe.sem_inc(turned, KB + 1)
            pe.wait_ge(w_in, 128)
            pe.wait_ge(cleared, 3)

            def group(i, s, nb):
                pe.wait_ge(attr_in[s], i * 16 + 16)
                for k in range(-(-nb // SB)):
                    u, q = i * (2 * KB) + (s * KB + k), (s * KB + k) % 2
                    pairs = min(SB // 2, -(-(nb - k * SB) // 2))
                    pe.wait_ge(turned_back, u + 1)
                    for m in range(pairs):
                        b = k * SB + 2 * m
                        last = pe.transpose(tp[q][0:2 * A, m * P:(m + 1) * P], attr[:, s, b:b + 2, :].rearrange("p b a -> p (b a)"), r.ident[:, :])
                    last.then_inc(turned, 1)
                    pe.wait_ge(turned_back, u + 3)
                    pe.wait_ge(act_done, u + 1)
                    pe.matmul(hp[q][0:2 * H, 0:pairs * P], lhsT=w1[:, :], rhs=attrT[:, q, 0:pairs * P], start=True, stop=True).then_inc(hid, 1)
                    pe.wait_ge(act_done, u + 3)
                    pe.wait_ge(gate_used, u + 1)
                    for m in range(pairs):
                        last = pe.matmul(gp_ps[q][:, m * 2 * H:(m + 1) * 2 * H], lhsT=hidden[:, q, m * P:(m + 1) * P], rhs=w2[:, :],
                                         start=True, stop=True)
                    last.then_inc(gated, 1)
            with pe.Fori(0, NI) as i:
                for s in range(2):
                    group(i, s, B)
            group(NI, 0, TAIL)

        @block.scalar
        def _(act):
            act.sem_inc(turned_back, 2)
            act.sem_inc(act_done, 2)
            act.wait_ge(w_in, 128)

            def group(i, s, nb):
                for k in range(-(-nb // SB)):
                    u, q = i * (2 * KB) + (s * KB + k), (s * KB + k) % 2
                    n = min(SB // 2, -(-(nb - k * SB) // 2)) * P
                    act.wait_ge(hid, u + 1)
                    act.wait_ge(turned, u + KB + 2)
                    act.activation(attrT[:, q, 0:n], tp[q][0:2 * A, 0:n], ACT.Copy).then_inc(turned_back, 1)
                    act.wait_ge(gated, u + 1)
                    act.wait_ge(hid, u + 3)
                    act.activation(hidden[0:2 * H, q, 0:n], hp[q][0:2 * H, 0:n], ACT.Silu, bias=b1[:, :]).then_inc(act_done, 1)
            with act.Fori(0, NI) as i:
                for s in range(2):
                    group(i, s, B)
            group(NI, 0, TAIL)

        @block.gpsimd
        def _(gp):
            gp.indirect_dma_start(row[:, 1, B - 1, :], None, d.rows1, bass.IndirectOffsetOnAxis(ap=r.first_dst[:, :], axis=0)).then_inc(first_row, 16)

            def scatter(s, nb):
                for b in range(nb):
                    gp.indirect_dma_start(d.records, bass.IndirectOffsetOnAxis(ap=slot[:, s, b:b + 1], axis=0), rec[:, s, b, :], None).then_inc(scattered[s], 16)
            with gp.Fori(0, NI) as i:
                for s in range(2):
                    gp.wait_ge(rec_ready, i * 2 + (s + 1))
                    gp.sem_inc(pool_go, 1)
                    scatter(s, B)
            gp.wait_ge(rec_ready, 2 * NI + 1)
            scatter(0, TAIL)
            gp.wait_ge(scattered[0], 16 * (NI * B + TAIL))
            gp.wait_ge(scattered[1], 16 * NI * B)

        @block.vector
        def _(v):
            step = Steps(v, dv)
            v.memset(w1[:, :], 0.0).then_inc(cleared, 1)
            v.memset(w2[:, :], 0.0).then_inc(cleared, 1)
            v.memset(hidden[2 * H:2 * H + 1, :, :], 1.0).then_inc(cleared, 1)
            v.sem_inc(spread_used, 2)
            v.sem_inc(emb_used, 2)
            v.sem_inc(gate_used, 2)
            step(v.memset(rec[:, :, :, :], 0.0))
            v.wait_ge(first_row, 16)

            def group(i, s, nb, first=False):
                g = i * 2 + s
                cols = bass.ds(g * B, nb)
                step(v.tensor_scalar(same[:, s, 0:nb], r.same[:, cols], 1.0, None, ALU.mult))
                v.wait_ge(spread_in[s], i * 16 + 16)
                for b in range(nb):
                    prev = row[:, s, b - 1, :] if b else row[:, 1 - s, B - 1, :]
                    step(v.scalar_tensor_tensor(row[:, s, b, :], prev, same[:, s, b:b + 1], spread[:, s, b, :], ALU.mult, ALU.add))
                v.sem_inc(spread_used, 1)
                v.wait_ge(emb_in[s], i * 16 + 16)
                step(v.tensor_tensor(prod[:, 0:nb, :], emb[:, s, 0:nb, :], row[:, s, 0:nb, H + 1:], ALU.mult))
                v.sem_inc(emb_used, 1)
                step(v.tensor_reduce(logit[:, 0:nb], prod[:, 0:nb, :], AX, ALU.add))
                step(v.tensor_tensor(coef[:, 0:nb], r.cut[:, cols], row[:, s, 0:nb, H], ALU.mult))
                if not first:
                    v.wait_ge(scattered[s], i * (16 * B))
                step(v.tensor_scalar(message[:, 0:nb, H], row[:, s, 0:nb, H], 1.0, None, ALU.mult))
                step(v.tensor_scalar(rec[:, s, 0:nb, WM], r.w[:, cols], 1.0, None, ALU.mult))
                step(v.tensor_scalar(rec[:, s, 0:nb, WM + 1], r.gidx[:, cols], 1.0, None, ALU.mult))
                step(v.tensor_scalar(lo[:, 0:nb], r.src[:, cols], P - 1, None, ALU.bitwise_and))
                step(v.tensor_scalar(rec[:, s, 0:nb, WM + 2], lo[:, 0:nb], 1.0, None, ALU.mult))
                step(v.tensor_scalar(slot[:, s, 0:nb], r.pos_i[:, cols], 0.0, None, ALU.add))
                for k in range(-(-nb // SB)):
                    u, q = i * (2 * KB) + (s * KB + k), (s * KB + k) % 2
                    n, b = min(SB, nb - k * SB), k * SB
                    v.wait_ge(gated, u + 3)
                    ins = v.tensor_tensor(gate[:, 0:n, :], gp_ps[q][:, 0:n * H].rearrange("p (b f) -> p b f", f=H),
                                          bc(logit[:, b:b + n].unsqueeze(2), 2, H), ALU.add)
                    step(ins)
                    v.sem_inc(gate_used, 1)
                    step(v.tensor_tensor(gate[:, 0:n, :], gate[:, 0:n, :], row[:, s, b:b + n, 0:H], ALU.mult))
                    step(v.tensor_tensor(message[:, b:b + n, 0:H], gate[:, 0:n, :], bc(coef[:, b:b + n].unsqueeze(2), 2, H), ALU.mult))
                for k in range(3):
                    part = thirds[:, s, 0:nb, k * (H + 1):(k + 1) * (H + 1)]
                    step(v.tensor_copy(part, message[:, 0:nb, :]))
                    if k < 2:
                        step(v.tensor_tensor(message[:, 0:nb, :], message[:, 0:nb, :], part, ALU.subtract))
                v.sem_inc(rec_ready, 1)
            for s in range(2):
                group(0, s, B, first=True)
            with v.Fori(1, NI) as i:
                step.enter(i - 1, 2 * (1 + B + 3 + 6 + 3 * KB + 5))
                for s in range(2):
                    group(i, s, B)
            step.leave(NI - 1)
            group(NI, 0, TAIL)


def tile_blocks(nc, c, sem):
    r = c.r
    W = 512
    assert r.offset.shape[1] % W == 0
    with (
        nc.sbuf_tensor("tb_tile", [P, T // BT * 16], I32) as tile,
        nc.sbuf_tensor("tb_ge", [P, T // BT * 16], F32) as ge,
        nc.sbuf_tensor("tb_first", [P, P], F32) as first,
        nc.psum_tensor("tb_ft", [P, 512], F32) as ft,
        nc.psum_tensor("tb_n", [P, 2, 512], F32) as cnt,
        nc.Block() as block,
    ):
        it, pt, dv = sem("tb_iota"), sem("tb_pe"), sem("tb_dve")

        @block.gpsimd
        def _(gp):
            gp.iota(tile[:, :], pattern=[[BT, T // BT], [2, 16]], base=0, channel_multiplier=0).then_inc(it, 1)

        @block.tensor
        def _(pe):
            pe.transpose(ft[:, 0:P], r.first_tile[:, :], r.ident[:, :]).then_inc(pt, 1)
            for k in range(r.offset.shape[1] // W):
                pe.wait_ge(dv, 2 if k < 2 else k + 1)
                pe.matmul(cnt[0:1, k % 2, 0:W], lhsT=r.ones[0:NB, 0:1], rhs=ge[0:NB, k * W:(k + 1) * W], start=True, stop=True).then_inc(pt, 1)

        @block.vector
        def _(v):
            step = Steps(v, dv)
            v.wait_ge(pt, 1)
            step(v.tensor_copy(first[:, :], ft[:, 0:P]))
            v.wait_ge(it, 1)
            step(v.tensor_scalar(ge[:, :], tile[:, :], first[:, 0:1], None, ALU.is_ge))
            for k in range(r.offset.shape[1] // W):
                v.wait_ge(pt, k + 2)
                step(v.tensor_scalar(r.offset[0:1, k * W:(k + 1) * W], cnt[0:1, k % 2, 0:W], -1.0, float(H + 1), ALU.add, ALU.mult))


def load_offsets(nc, v, offset, g):
    _, vals = nc.values_load_multi_w_load_instructions(
        offset[0:1, bass.ds(g * 16, BT // 2)], engines=[v.engine], min_val=0, max_val=(NB - 1) * (H + 1),
        skip_runtime_bounds_check_because="a block's number times a row's width, from tile_blocks")
    return vals


def sum_by_src(nc, c, sem, name, table, accs, width):
    d, r = c.d, c.r
    lay1 = table is None
    lanes = len(accs)
    RS = 4 if lay1 else 2
    TURNS = T // BT // RS
    HT = BT // 2
    assert TURNS * RS * BT == T
    with ExitStack() as ctx:
        sb = lambda n, s, t=F32: ctx.enter_context(nc.sbuf_tensor(name + n, s, t))
        ring = sb("ring", [P, RS, BT, WR if lay1 else H])
        hot = sb("hot", [P, 4, HT, P], BF16 if lay1 else F32)
        parts = ring[:, :, :, 0:WM].bitcast(BF16) if lay1 else ring
        NPARTS = 3 if lay1 else 1
        banks = [[ctx.enter_context(nc.psum_tensor(f"{name}ps{s}{k}", [P, 512], F32)) for k in range(2)] for s in range(2)]
        landed = [sem(f"{name}_landed{q}") for q in range(RS)]
        hot_ready = [sem(f"{name}_hot_ready{half}") for half in range(2)]
        free, summed, kept, go, dv, idx_ready, abs_done, sp_go = (
            sem(f"{name}_{n}") for n in ("free", "summed", "kept", "go", "dve", "idx_ready", "abs_done", "sp_go"))
        if not lay1:
            idx, small = sb("idx", [P, 2, BT], I32), sb("small", [P, 2, BT])
        block = ctx.enter_context(nc.Block())

        def sums(s, k):
            return banks[s][k // 10][:, k % 10 * width:(k % 10 + 1) * width]

        def groups(eng, body):
            with eng.Fori(0, TURNS) as i:
                for q in range(RS):
                    body(i, q, i * RS + q)

        if lay1:
            @block.sync
            def _(sp):
                rec_v = d.records.rearrange("(p j) c -> p j c", p=P)

                def load(i, q, g):
                    halves = g * 2 + 2
                    sp.wait_ge(summed, halves)
                    sp.wait_ge(kept, halves)
                    sp.sem_inc(sp_go, 1)
                    sp.dma_start(ring[:, q, :, :], rec_v[:, bass.ds(g * BT, BT), :]).then_inc(landed[q], 16)
                groups(sp, load)
                load(TURNS, 0, TURNS * RS)
                for q in range(RS):
                    sp.wait_ge(landed[q], 16 * (TURNS + (q == 0)))

            @block.scalar
            def _(act):
                act.sem_inc(kept, 2 * RS)

                def finish(i, q, g):
                    act.wait_ge(landed[q], i * 16 + 16)
                    act.wait_ge(summed, i * (2 * RS) + (2 * q + 6))
                    for k in range(HT):
                        last = act.activation(hot[:, 2 * (q % 2) + 1, k, :], r.iota[:, :], ACT.Abs, bias=ring[:, q, HT + k, WM + 2:WM + 3], scale=-1.0)
                    last.then_inc(abs_done, 1)
                    cols = bass.ds(g * BT, BT)
                    act.activation(r.w3[:, cols], ring[:, q, :, WM], ACT.Copy)
                    act.activation(r.row3[:, cols], ring[:, q, :, WM + 1], ACT.Copy)
                    act.activation(r.lo3[:, cols], ring[:, q, :, WM + 2], ACT.Copy).then_inc(kept, 2)
                    act.wait_ge(abs_done, i * RS + (q + 1))
                    flat = hot[:, 2 * (q % 2) + 1, :, :].rearrange("p b f -> p (b f)")
                    act.activation(flat, flat, ACT.Relu, bias=1.0, scale=-1.0).then_inc(hot_ready[1], 1)
                groups(act, finish)
        else:
            @block.gpsimd
            def _(gp):
                def gather(i, q, g):
                    gp.wait_ge(idx_ready, i * RS + (q + 1))
                    gp.sem_inc(go, 1)
                    for b in range(BT):
                        gp.indirect_dma_start(ring[:, q, b, :], None, table,
                                              bass.IndirectOffsetOnAxis(ap=idx[:, q, b:b + 1], axis=0)).then_inc(landed[q], 16)
                groups(gp, gather)

        @block.tensor
        def _(pe):
            pe.sem_inc(summed, 8)

            def products(i, q, g):
                pe.wait_ge(landed[q], (i + 1) * (16 if lay1 else 16 * BT))
                pe.wait_ge(free, g + 1)
                for half in range(2):
                    pe.wait_ge(hot_ready[half], g + 1)
                    for k in range(HT):
                        b = half * HT + k
                        for part in range(NPARTS):
                            last = pe.matmul(sums(q % 2, b // 2), lhsT=hot[:, 2 * (q % 2) + half, k, :],
                                             rhs=parts[:, q, b, part * width:(part + 1) * width],
                                             start=b % 2 == 0 and part == 0, stop=b % 2 == 1 and part == NPARTS - 1)
                    last.then_inc(summed, 1)
            groups(pe, products)

        @block.vector
        def _(v):
            step = Steps(v, dv)
            v.sem_inc(free, 2)

            def onehots(i, q, g):
                if lay1:
                    v.wait_ge(landed[q], i * 16 + 16)
                    v.tensor_tensor(hot[:, 2 * (q % 2), :, :], bc(r.iota[:, :].unsqueeze(1), 1, HT), bc(ring[:, q, 0:HT, WM + 2:WM + 3], 2, P),
                                    ALU.is_equal).then_inc(hot_ready[0], 1)
                    return
                step(v.tensor_scalar(small[:, 0, :], r.lo3[:, bass.ds(g * BT, BT)], 1.0, None, ALU.mult))
                step(v.tensor_scalar(small[:, 1, :], r.w3[:, bass.ds(g * BT, BT)], 1.0, None, ALU.mult))
                for half in range(2):
                    for k in range(HT):
                        b = half * HT + k
                        last = v.tensor_scalar(hot[:, 2 * q + half, k, :], r.iota[:, :], small[:, 0, b:b + 1], small[:, 1, b:b + 1],
                                               ALU.is_equal, ALU.mult)
                    last.then_inc(hot_ready[half], 1)
                v.wait_ge(hot_ready[1], g + 1)

            def stage(g, s):
                v.tensor_scalar(idx[:, s, :], r.row3[:, bass.ds(g * BT, BT)], 0.0, None, ALU.add).then_inc(idx_ready, 1)

            for part in accs:
                step(v.memset(part[:, :, :], 0.0))
            flat = [part[:, :, :].rearrange("p b f -> p (b f)") for part in accs]
            if not lay1:
                for q in (r.w3, r.lo3):
                    step(v.memset(q[:, T:], 0.0))
                step(v.memset(r.row3[:, T:], 0))
                for s in range(2):
                    stage(s, s)
            onehots(0, 0, 0)

            def add(i, q, g):
                onehots(i + (q + 1) // RS, (q + 1) % RS, g + 1)
                offs = load_offsets(nc, v, r.offset, g)
                v.wait_ge(summed, g * 2 + 10)
                for k in range(BT // 2):
                    part = flat[k % lanes][:, bass.ds(offs[k], width)]
                    v.tensor_tensor(part, part, sums(q % 2, k), ALU.add).then_inc(dv, 1)
                    step.wait_last(behind=0 if k == BT // 2 - 1 else lanes - 1)
                v.sem_inc(free, 1)
                if not lay1:
                    stage(g + 2, q)
            with v.Fori(0, TURNS) as i:
                step.enter(i, RS * (BT // 2 + (0 if lay1 else 2)))
                for q in range(RS):
                    add(i, q, i * RS + q)
            step.leave(TURNS)


def layer1_finish(nc, c, sem, acc):
    d, r = c.d, c.r
    with ExitStack() as ctx:
        sb = lambda n, s, t=F32: ctx.enter_context(nc.sbuf_tensor("f1" + n, s, t))
        stat, y, vec, w = sb("stat", [P, 4, NB]), sb("y", [P, NB, H]), sb("vec", [P, 2, H]), sb("w", [H, H])
        acc, acc2 = acc
        tmp = acc[:, :, 0:H]
        ld, dv, ready, rt, done, wr = (sem("f1_" + n) for n in ("w_in", "dve", "var", "root", "done", "written"))
        prod = NodeProduct(nc, ctx, sem, "n2", w[:, :], H)
        block = ctx.enter_context(nc.Block())

        @block.sync
        def _(sp):
            sp.dma_start(vec[:, 0, :], bcast_row(d.gamma)).then_inc(ld, 16)
            sp.dma_start(vec[:, 1, :], bcast_row(d.beta)).then_inc(ld, 16)
            sp.dma_start(w[:, :], d.W_2).then_inc(ld, 16)
            sp.wait_ge(ld, 48)
            sp.wait_ge(done, 1)
            sp.dma_start(nodes(d.rows2), r.a[:, :, :]).then_inc(wr, 16)
            sp.wait_ge(wr, 16)

        @block.vector
        def _(v):
            step = Steps(v, dv)
            step(v.tensor_tensor(acc[:, :, :], acc[:, :, :], acc2[:, :, :], ALU.add))
            step(v.tensor_scalar(stat[:, 0, :], acc[:, :, H], 1e-8, None, ALU.max))
            step(v.reciprocal(stat[:, 0, :], stat[:, 0, :]))
            step(v.tensor_tensor(y[:, :, :], acc[:, :, 0:H], bc(stat[:, 0, :].unsqueeze(2), 2, H), ALU.mult))
            step(v.tensor_tensor(r.a[:, :, :], r.a[:, :, :], y[:, :, :], ALU.add))
            layernorm_relu(nc, v, step, (rt, 1), ready, y[:, :, :], r.a[:, :, :], tmp, stat, relu=False)
            v.wait_ge(ld, 48)
            step(v.tensor_tensor(y[:, :, :], y[:, :, :], bc(vec[:, 0:1, :], 1, NB), ALU.mult))
            step(v.tensor_tensor(y[:, :, :], y[:, :, :], bc(vec[:, 1:2, :], 1, NB), ALU.add))
            step(v.tensor_tensor(r.x[:, :, :], r.x[:, :, :], y[:, :, :], ALU.add))
            step(v.tensor_scalar(stat[:, 1, :], r.deg[:, :], 1.0, None, ALU.add))
            v.sem_inc(ready, 1)
            v.wait_ge(rt, 2)
            step(v.reciprocal(r.dinv[:, :], stat[:, 2, :]))
            layernorm_relu(nc, v, step, (rt, 3), ready, r.a[:, :, :], r.x[:, :, :], tmp, stat)

            def take(g, s, nb, rows):
                return v.tensor_tensor(r.a[:, bass.ds(g * prod.CB, nb), :], rows[0], bc(r.dinv[:, bass.ds(g * prod.CB, nb)].unsqueeze(2), 2, H), ALU.mult)
            prod.on_vector(v, r.a, take)
            v.sem_inc(done, 1)

        @block.scalar
        def _(act):
            for k in range(3):
                root(nc, act, ready, k + 1, rt, stat)
            prod.on_scalar(act)

        @block.tensor
        def _(pe):
            pe.wait_ge(ld, 48)
            prod.on_tensor(pe, r.ident)


def layer2_finish(nc, c, sem):
    d, r = c.d, c.r
    with ExitStack() as ctx:
        sb = lambda n, s, t=F32: ctx.enter_context(nc.sbuf_tensor("f2" + n, s, t))
        took = sb("took", [P, NB, H])
        mend_and_take(nc, c, sem, "m2", d.state2, False, r.ends, took)
        stat, b, w = sb("stat", [P, 4, NB]), sb("b", [P, 1, H]), sb("w", [H, NR * H])
        y = sb("y", [P, 2, NodeProduct.CB, NR * H])
        ld, dv, ready, rt = (sem("f2_" + n) for n in ("w_in", "dve", "var", "root"))
        wr = [sem(f"f2_written{s}") for s in range(2)]
        prod = NodeProduct(nc, ctx, sem, "n3", w[:, :], NR * H)
        block = ctx.enter_context(nc.Block())

        @block.sync
        def _(sp):
            sp.dma_start(w[:, :].rearrange("i (r o) -> i r o", r=NR), d.W_3.rearrange("(r i) o -> i r o", r=NR)).then_inc(ld, 16)
            sp.dma_start(b[:, 0, :], bcast_row(d.b_2)).then_inc(ld, 16)
            sp.wait_ge(ld, 32)
            rows_v = d.rows3.rearrange("(b p r) c -> p b (r c)", p=P, r=NR)
            for s in range(2):
                sp.sem_inc(wr[s], 16)

            def chunk(g, s, nb):
                sp.wait_ge(prod.taken, g + 3)
                sp.dma_start(rows_v[:, bass.ds(g * prod.CB, nb), :], y[:, s, 0:nb, :]).then_inc(wr[s], 16)
            prod.chunks(sp, chunk)
            sp.wait_ge(wr[0], 16 * (prod.TURNS + 2))
            sp.wait_ge(wr[1], 16 * (prod.TURNS + 1))

        @block.vector
        def _(v):
            step = Steps(v, dv)
            has = stat[:, 0, :]
            step(v.tensor_scalar(has, r.deg[:, :], 0.0, None, ALU.is_gt))
            step(v.tensor_tensor(took[:, :, :], took[:, :, :], bc(has.unsqueeze(2), 2, H), ALU.mult))
            step(v.tensor_tensor(r.a[:, :, :], r.a[:, :, :], took[:, :, :], ALU.add))
            step(v.tensor_tensor(r.a[:, :, :], r.a[:, :, :], bc(r.dinv[:, :].unsqueeze(2), 2, H), ALU.mult))
            v.wait_ge(ld, 32)
            step(v.tensor_tensor(r.a[:, :, :], r.a[:, :, :], bc(b[:, :, :], 1, NB), ALU.add))
            step(v.tensor_tensor(r.x[:, :, :], r.x[:, :, :], r.a[:, :, :], ALU.add))
            layernorm_relu(nc, v, step, (rt, 1), ready, r.a[:, :, :], r.x[:, :, :], took[:, :, :], stat)

            def take(g, s, nb, rows):
                v.wait_ge(wr[s], (g - s) * 8 + 16)
                for k, part in enumerate(rows):
                    n = part.shape[1]
                    last = v.tensor_copy(y[:, s, k * prod.per:k * prod.per + n, :], part)
                return last
            prod.on_vector(v, r.a, take)

        @block.scalar
        def _(act):
            root(nc, act, ready, 1, rt, stat)
            prod.on_scalar(act)

        @block.tensor
        def _(pe):
            pe.wait_ge(ld, 32)
            prod.on_tensor(pe, r.ident)


def layer3_finish(nc, c, sem, acc):
    d, r = c.d, c.r
    ld, dv = sem("f3_b_in"), sem("f3_dve")
    with nc.sbuf_tensor("f3b", [P, 1, H], F32) as b, nc.Block() as block:
        @block.sync
        def _(sp):
            sp.dma_start(b[:, 0, :], bcast_row(d.b_3)).then_inc(ld, 16)
            sp.wait_ge(ld, 16)

        @block.vector
        def _(v):
            step = Steps(v, dv)
            step(v.tensor_tensor(r.x[:, :, :], r.x[:, :, :], acc[:, :, 0:H], ALU.add))
            v.wait_ge(ld, 16)
            step(v.tensor_tensor(r.x[:, :, :], r.x[:, :, :], bc(b[:, :, :], 1, NB), ALU.add))


def gnn(nc, x, src, dst, edge_attr_40, edge_type_4, edge_weight, node_type_119, node_vec, theta_w, theta_b, phi_w, phi_b,
        W1, b1, W2, b2, emb, adaptW, gamma, beta, W_2, b_2, W_3, b_3, out, stop=None):
    c = Shared()
    c.d, c.r = d, r = Shared(), Shared()
    d.x, d.src, d.dst, d.attr, d.edge_type, d.edge_weight, d.node_type, d.node_vec = (
        x, src, dst, edge_attr_40, edge_type_4, edge_weight, node_type_119, node_vec)
    d.theta_w, d.theta_b, d.phi_w, d.phi_b, d.emb, d.adaptW = theta_w, theta_b, phi_w, phi_b, emb, adaptW
    d.W1, d.b1, d.W2, d.b2, d.gamma, d.beta, d.W_2, d.b_2, d.W_3, d.b_3, d.out = W1, b1, W2, b2, gamma, beta, W_2, b_2, W_3, b_3, out

    def dram(name, shape):
        return nc.dram_tensor(name, shape, F32, kind="Internal").ap()
    d.rows0 = dram("rows0_dram", (NP, W0))
    d.emb_edge = dram("emb_edge_dram", (E, EM))
    d.state = dram("state0_dram", (E + P, H))
    d.state2 = dram("state2_dram", (E + P, H))
    d.spread = dram("spread_dram", (SR * P, WX))
    d.records = dram("records_dram", (XR * P, WR))
    d.rows1 = dram("rows1_dram", (NP, WX))
    d.rows2 = dram("rows2_dram", (NP, H))
    d.rows3 = dram("rows3_dram", (NP * NR, H))

    d.attr_sorted = dram("attr_sorted_dram", (E, A))
    d.sorted_records = [dram(f"sorted{k}_dram", (E, 8)) for k in range(2)]

    with ExitStack() as ctx:
        ctx.enter_context(nc.allow_non_contiguous_dma("small loads, one value at a time"))

        used = []

        def sem(name):
            used.append(nc.alloc_semaphore(name=name))
            return used[-1]

        def renew_semaphores():
            nc.clear_and_free_semaphores(used)
            nc.all_engine_barrier()
            used.clear()

        def res(name, shape, t=F32):
            return ctx.enter_context(nc.sbuf_tensor("r_" + name, shape, t))
        r.src, r.same = res("src", [P, JP], I32), res("same", [P, J])
        dst_and_e2 = res("dst_and_e2", [P, J + 1 + NB * EM])
        r.dst = dst_and_e2[:, 0:J + 1].bitcast(I32)
        r.w3, r.lo3, r.row3 = res("w", [P, TP]), res("gidx", [P, TP]), res("pos", [P, TP], I32)
        r.w, r.gidx, r.pos_i = r.w3[:, 0:J], r.lo3[:, 0:J], r.row3[:, 0:J]
        r.gidx_i, r.pos = r.pos_i, r.pos_i.bitcast(F32)
        r.x, r.a, r.mult = res("x", [P, NB, H]), res("a", [P, NB, H]), res("mult", [P, NB])
        r.e2 = dst_and_e2[:, J + 1:].rearrange("p (b f) -> p b f", b=NB)
        r.ident, r.ones, r.before, r.iota, r.iota16 = (res("ident", [P, P]), res("ones", [P, P]), res("before", [P, P]), res("iota", [P, P]),
                                                       res("iota16", [P, P], BF16))
        r.part, r.full, r.first_tile, r.deg = res("part", [P, 1]), res("full", [H, P]), res("first_tile", [P, P]), res("deg", [P, NB])
        r.mend_read, r.mend_write, r.first_dst = res("mend_read", [P, 1], I32), res("mend_write", [P, 1], I32), res("first_dst", [P, 1], I32)
        r.unsorted = res("unsorted", [P, 1], I32)
        r.dinv = res("dinv", [P, NB])
        r.ends, r.starts = res("ends", [P, NB], I32), res("starts", [P, NB], I32)
        r.cut = dst_and_e2[:, 0:J]
        load_resident(nc, c, sem)
        unsorted = nc.values_load(r.unsorted[0:1, 0:1], min_val=0, max_val=1)
        with nc.If(unsorted > 0):
            sort_by_dst(nc, c, sem)
        renew_semaphores()
        first_segments(nc, c, sem)
        layer0_tables(nc, c, sem)
        gather_reduce(nc, c, sem, "g0", d.rows0, W0, d.state, True)
        rows_of_dst(nc, c, sem)
        layer0_finish(nc, c, sem)
        if stop == 0:
            return store_x(nc, c, sem)
        layer1_edges(nc, c, sem)
        r.offset = res("offset", [1, T // BT * 16], I32)
        tile_blocks(nc, c, sem)
        with nc.sbuf_tensor("acc1", [P, NB, H + 1], F32) as acc_even:
            acc = (acc_even, dst_and_e2[:, 0:NB * (H + 1)].rearrange("p (b f) -> p b f", b=NB))
            sum_by_src(nc, c, sem, "s1", None, acc, H + 1)
            layer1_finish(nc, c, sem, acc)
        if stop == 1:
            return store_x(nc, c, sem)
        renew_semaphores()
        gather_reduce(nc, c, sem, "g2", d.rows2, H, d.state2, False)
        layer2_finish(nc, c, sem)
        if stop == 2:
            return store_x(nc, c, sem)
        with nc.sbuf_tensor("acc3", [P, NB, H + 1], F32) as acc:
            sum_by_src(nc, c, sem, "s3", d.rows3, (acc,), H)
            layer3_finish(nc, c, sem, acc)
        store_x(nc, c, sem)


_INS = ['x', 'src', 'dst', 'edge_attr_40', 'edge_type_4', 'edge_weight', 'node_type_119', 'node_vec', 'L0_gnn_theta_w',
        'L0_gnn_theta_b', 'L0_gnn_phi_w', 'L0_gnn_phi_b', 'L1_gnn_W1', 'L1_gnn_b1', 'L1_gnn_W2', 'L1_gnn_b2', 'L1_gnn_emb',
        'L1_gnn_adaptW', 'L1_gnn_gamma', 'L1_gnn_beta', 'L2_gnn_W', 'L2_gnn_b', 'L3_gnn_W', 'L3_gnn_b']
_OUTS = [((12500, 48), 'float32')]


def kernel(**inputs):
    import numpy as _np
    import concourse.bacc as _bacc
    from concourse import mybir as _mybir
    from concourse.bass_utils import run_bass_kernel_spmd as _run

    nc = _bacc.Bacc("TRN2", target_bir_lowering=False, num_devices=1)
    arrays, args = {}, []
    for name in _INS:
        a = _np.ascontiguousarray(inputs[name])
        arrays[f"in_{name}_dram"] = a
        args.append(nc.dram_tensor(f"in_{name}_dram", a.shape, _mybir.dt.from_np(a.dtype), kind="ExternalInput").ap())
    for i, (shape, dtype) in enumerate(_OUTS):
        dt = _mybir.dt.from_np(_np.dtype(dtype))
        args.append(nc.dram_tensor(f"out_{i}_dram", shape, dt, kind="ExternalOutput").ap())
    gnn(nc, *args)
    r = _run(nc, [arrays], core_ids=[0])
    got = tuple(r.results[0][f"out_{i}_dram"] for i in range(len(_OUTS)))
    return got[0]
```
